# Optimizing a Trainium2 kernel written in Bass

```python
import numpy as np
import jax
import jax.numpy as jnp

def _softmax(x, axis=-1):
    return jax.nn.softmax(x, axis=axis)

def _gelu(x):
    return jax.nn.gelu(x, approximate=True)

def _silu(x):
    return jax.nn.silu(x)

def _sigmoid(x):
    return jax.nn.sigmoid(x)

def _layernorm(x, axis=-1, eps=1e-05):
    m = jnp.mean(x, axis=axis, keepdims=True)
    v = jnp.var(x, axis=axis, keepdims=True)
    return (x - m) / jnp.sqrt(v + eps)

def _scatter_add(tgt, idx, src, axis=0):
    return tgt.at[idx].add(src)

def _segment_sum(src, seg, n):
    return jax.ops.segment_sum(src, seg, n)
kernel_name = 'mk_adaln_ffn_d2_seqx_r8_43008f'

def setup_inputs(seed: int=0):
    np.random.seed(seed)
    _w = jnp.asarray

    def _rec_inputs():
        import jax
        import jax.numpy as jnp
        _rk = jax.random.key(seed)
        x = -0.0003929 + 0.9999 * jax.random.normal(jax.random.fold_in(_rk, 1), (16, 128, 128), jnp.float32)
        _lenS = 128 - jax.random.randint(jax.random.fold_in(_rk, 7), (16,), 0, max(1, 128 // 4) + 1, jnp.int32)
        _lenS2 = 128 - jax.random.randint(jax.random.fold_in(_rk, 8), (16,), 0, max(1, 128 // 4) + 1, jnp.int32)
        fside_Bx1x1024x16_0 = 0.00222621 + 0.99962 * jax.random.normal(jax.random.fold_in(_rk, 11), (16, 1, 128, 16), jnp.float32)
        cond_1024 = -0.00745576 + 0.997402 * jax.random.normal(jax.random.fold_in(_rk, 12), (16, 128), jnp.float32)
        return (x, fside_Bx1x1024x16_0, cond_1024)
    x, fside_Bx1x1024x16_0, cond_1024 = _rec_inputs()

    def _L0_cond_setup():
        import jax, jax.numpy as jnp
        import numpy as np
        B, F_, IN, OUT, R = (32, 64, 128, 128, 16)
        key = jax.random.key(seed)
        ks = jax.random.split(key, 6)
        x = jax.random.normal(ks[0], (B, F_, IN), dtype=jnp.float32)
        u = jax.random.normal(ks[1], (B, 1, OUT, R), dtype=jnp.float32)
        v = jax.random.normal(ks[2], (B, 1, IN, R), dtype=jnp.float32)
        b = jax.random.normal(ks[3], (B, 1, OUT), dtype=jnp.float32)
        lim = 1.0 / np.sqrt(IN)
        W = jax.random.uniform(ks[4], (OUT, IN), minval=-lim, maxval=lim, dtype=jnp.float32)
        fc_bias = jax.random.uniform(ks[5], (OUT,), minval=-lim, maxval=lim, dtype=jnp.float32)
        return {'x': x, 'u': u, 'v': v, 'b': b, 'W': W, 'fc_bias': fc_bias}
    _L0_cond_all = _L0_cond_setup()
    _L0_cond_in = {k: v for k, v in _L0_cond_all.items() if k in ('W', 'fc_bias')}
    del _L0_cond_all

    def _L0_ffn_setup():
        import jax, jax.numpy as jnp
        import numpy as np
        EPS = 1e-05

        def _quantize(W):
            gamma = jnp.mean(jnp.abs(W))
            return jnp.clip(jnp.round(W / (gamma + EPS)), -1.0, 1.0)
        key = jax.random.key(seed)
        k_x, k_w1, k_b1, k_w2, k_b2 = jax.random.split(key, 5)
        n_embd = 128
        d_ff = 4 * n_embd
        B, S = (4, 512)
        bound1 = 1.0 / np.sqrt(n_embd)
        bound2 = 1.0 / np.sqrt(d_ff)
        x = jax.random.normal(k_x, (B, S, n_embd), dtype=jnp.float32)
        W1 = jax.random.uniform(k_w1, (d_ff, n_embd), jnp.float32, -bound1, bound1)
        b1 = jax.random.uniform(k_b1, (d_ff,), jnp.float32, -bound1, bound1)
        W2 = jax.random.uniform(k_w2, (n_embd, d_ff), jnp.float32, -bound2, bound2)
        b2 = jax.random.uniform(k_b2, (n_embd,), jnp.float32, -bound2, bound2)
        return {'x': x, 'W1': W1, 'b1': b1, 'W2': W2, 'b2': b2}
    _L0_ffn_all = _L0_ffn_setup()
    _L0_ffn_in = {k: v for k, v in _L0_ffn_all.items() if k in ('W1', 'b1', 'W2', 'b2')}
    del _L0_ffn_all

    def _L1_cond_setup():
        import jax, jax.numpy as jnp
        import numpy as np
        B, T, C = (64, 64, 128)
        key = jax.random.key(seed)
        ks = jax.random.split(key, 17)
        s_in = 1.0 / np.sqrt(C)

        def lin(kw, kb, fan_in):
            s = 1.0 / np.sqrt(fan_in)
            W = jax.random.uniform(kw, (C, fan_in), jnp.float32, -s, s)
            b = jax.random.uniform(kb, (C,), jnp.float32, -s, s)
            return (W, b)
        Wxz, bxz = lin(ks[0], ks[1], C)
        Whz, bhz = lin(ks[2], ks[3], C)
        Wxr, bxr = lin(ks[4], ks[5], C)
        Whr, bhr = lin(ks[6], ks[7], C)
        Wxh, bxh = lin(ks[8], ks[9], C)
        Whh, bhh = lin(ks[10], ks[11], C)
        Whq, bhq = lin(ks[12], ks[13], C)
        X = jax.random.normal(ks[14], (B, T, C), jnp.float32)
        h0 = jax.random.normal(ks[15], (B, C), jnp.float32)
        return {'X': X, 'h0': h0, 'Wxz': Wxz, 'bxz': bxz, 'Whz': Whz, 'bhz': bhz, 'Wxr': Wxr, 'bxr': bxr, 'Whr': Whr, 'bhr': bhr, 'Wxh': Wxh, 'bxh': bxh, 'Whh': Whh, 'bhh': bhh, 'Whq': Whq, 'bhq': bhq}
    _L1_cond_all = _L1_cond_setup()
    _L1_cond_in = {k: v for k, v in _L1_cond_all.items() if k in ('Wxz', 'bxz', 'Whz', 'bhz', 'Wxr', 'bxr', 'Whr', 'bhr', 'Wxh', 'bxh', 'Whh', 'bhh', 'Whq', 'bhq')}
    del _L1_cond_all

    def _L1_ffn_setup():
        import jax, jax.numpy as jnp
        import numpy as np
        B, K, D = (128, 32, 128)
        E = 32
        H = int(D * 0.25)

        def _rsqrt_uniform(key, shape, d):
            bound = d ** (-0.5)
            return jax.random.uniform(key, shape, jnp.float32, -bound, bound)
        key = jax.random.key(seed)
        ks = jax.random.split(key, 7)
        return {'x': jax.random.normal(ks[0], (B, K, D), jnp.float32), 'router_w': _rsqrt_uniform(ks[1], (E, D), D), 'router_b': _rsqrt_uniform(ks[2], (E,), D), 'weights1': _rsqrt_uniform(ks[3], (E, D, H), H), 'bias1': _rsqrt_uniform(ks[4], (E, H), H), 'weights2': _rsqrt_uniform(ks[5], (E, H, D), D), 'bias2': _rsqrt_uniform(ks[6], (E, D), D)}
    _L1_ffn_all = _L1_ffn_setup()
    _L1_ffn_in = {k: v for k, v in _L1_ffn_all.items() if k in ('router_w', 'router_b', 'weights1', 'bias1', 'weights2', 'bias2')}
    del _L1_ffn_all
    return {'x': x, 'fside_Bx1x1024x16_0': fside_Bx1x1024x16_0, 'cond_1024': cond_1024, 'L0_cond_W': _L0_cond_in['W'], 'L0_cond_fc_bias': _L0_cond_in['fc_bias'], 'L0_ffn_W1': _L0_ffn_in['W1'], 'L0_ffn_b1': _L0_ffn_in['b1'], 'L0_ffn_W2': _L0_ffn_in['W2'], 'L0_ffn_b2': _L0_ffn_in['b2'], 'L1_cond_Wxz': _L1_cond_in['Wxz'], 'L1_cond_bxz': _L1_cond_in['bxz'], 'L1_cond_Whz': _L1_cond_in['Whz'], 'L1_cond_bhz': _L1_cond_in['bhz'], 'L1_cond_Wxr': _L1_cond_in['Wxr'], 'L1_cond_bxr': _L1_cond_in['bxr'], 'L1_cond_Whr': _L1_cond_in['Whr'], 'L1_cond_bhr': _L1_cond_in['bhr'], 'L1_cond_Wxh': _L1_cond_in['Wxh'], 'L1_cond_bxh': _L1_cond_in['bxh'], 'L1_cond_Whh': _L1_cond_in['Whh'], 'L1_cond_bhh': _L1_cond_in['bhh'], 'L1_cond_Whq': _L1_cond_in['Whq'], 'L1_cond_bhq': _L1_cond_in['bhq'], 'L1_ffn_router_w': _L1_ffn_in['router_w'], 'L1_ffn_router_b': _L1_ffn_in['router_b'], 'L1_ffn_weights1': _L1_ffn_in['weights1'], 'L1_ffn_bias1': _L1_ffn_in['bias1'], 'L1_ffn_weights2': _L1_ffn_in['weights2'], 'L1_ffn_bias2': _L1_ffn_in['bias2']}

def reference(x, fside_Bx1x1024x16_0, cond_1024, L0_cond_W, L0_cond_fc_bias, L0_ffn_W1, L0_ffn_b1, L0_ffn_W2, L0_ffn_b2, L1_cond_Wxz, L1_cond_bxz, L1_cond_Whz, L1_cond_bhz, L1_cond_Wxr, L1_cond_bxr, L1_cond_Whr, L1_cond_bhr, L1_cond_Wxh, L1_cond_bxh, L1_cond_Whh, L1_cond_bhh, L1_cond_Whq, L1_cond_bhq, L1_ffn_router_w, L1_ffn_router_b, L1_ffn_weights1, L1_ffn_bias1, L1_ffn_weights2, L1_ffn_bias2):
    import jax
    import jax.numpy as jnp

    def _L0_cond_ref(x, u, v, b, W, fc_bias):
        import jax, jax.numpy as jnp
        import numpy as np
        B, F_, IN, OUT, R = (32, 64, 128, 128, 16)
        inch = x.shape[-1]
        r = v.shape[-1]
        z1 = jnp.einsum('bfi,bir->bfr', x, v[:, 0]) / inch
        z = jnp.einsum('bfr,bor->bfo', z1, u[:, 0]) / r
        y = jnp.einsum('bfi,oi->bfo', x, W) + fc_bias + z + b
        return jax.nn.gelu(y, approximate=False)

    def _L0_ffn_ref(x, W1, b1, W2, b2):
        import jax, jax.numpy as jnp
        import numpy as np
        EPS = 1e-05

        def _quantize(W):
            gamma = jnp.mean(jnp.abs(W))
            return jnp.clip(jnp.round(W / (gamma + EPS)), -1.0, 1.0)
        Wq1 = _quantize(W1)
        Wq2 = _quantize(W2)
        h = jax.nn.relu(jnp.einsum('bsd,fd->bsf', x, Wq1) + b1)
        out = jnp.einsum('bsf,df->bsd', h, Wq2) + b2
        return out

    def _L1_cond_ref(X, h0, Wxz, bxz, Whz, bhz, Wxr, bxr, Whr, bhr, Wxh, bxh, Whh, bhh, Whq, bhq):
        import jax, jax.numpy as jnp
        import numpy as np
        B, T, C = (64, 64, 128)
        Xz = jnp.einsum('btc,hc->tbh', X, Wxz) + bxz
        Xr = jnp.einsum('btc,hc->tbh', X, Wxr) + bxr
        Xh = jnp.einsum('btc,hc->tbh', X, Wxh) + bxh

        def step(H, xs):
            xz, xr, xh = xs
            Z = jax.nn.sigmoid(xz + H @ Whz.T + bhz)
            R = jax.nn.sigmoid(xr + H @ Whr.T + bhr)
            H_tilda = jnp.tanh(xh + R * H @ Whh.T + bhh)
            H_new = Z * H + (1.0 - Z) * H_tilda
            Y = H_new @ Whq.T + bhq
            return (H_new, Y)
        _, Ys = jax.lax.scan(step, h0, (Xz, Xr, Xh))
        return jnp.transpose(Ys, (1, 0, 2))

    def _L1_ffn_ref(x, router_w, router_b, weights1, bias1, weights2, bias2):
        import jax, jax.numpy as jnp
        import numpy as np
        B, K, D = (128, 32, 128)
        E = 32
        H = int(D * 0.25)

        def _rsqrt_uniform(key, shape, d):
            bound = d ** (-0.5)
            return jax.random.uniform(key, shape, jnp.float32, -bound, bound)
        b, k, d = x.shape
        x_flat = x.reshape(-1, d)
        n = x_flat.shape[0]
        logits = x_flat @ router_w.T + router_b
        routed_idx = jnp.argmax(logits, axis=-1)

        def expert_mlp(w1, b1, w2, b2):
            h = jax.nn.relu(x_flat @ w1 + b1)
            return jax.nn.relu(h @ w2 + b2)
        y_all = jax.vmap(expert_mlp)(weights1, bias1, weights2, bias2)
        out_flat = y_all[routed_idx, jnp.arange(n)]
        return out_flat.reshape(b, k, d)
    x = x + _L0_ffn_ref(_L0_cond_ref(x, fside_Bx1x1024x16_0, fside_Bx1x1024x16_0, cond_1024[:, None, :], L0_cond_W, L0_cond_fc_bias), L0_ffn_W1, L0_ffn_b1, L0_ffn_W2, L0_ffn_b2)
    x = x + _L1_ffn_ref(_L1_cond_ref(x, cond_1024, L1_cond_Wxz, L1_cond_bxz, L1_cond_Whz, L1_cond_bhz, L1_cond_Wxr, L1_cond_bxr, L1_cond_Whr, L1_cond_bhr, L1_cond_Wxh, L1_cond_bxh, L1_cond_Whh, L1_cond_bhh, L1_cond_Whq, L1_cond_bhq), L1_ffn_router_w, L1_ffn_router_b, L1_ffn_weights1, L1_ffn_bias1, L1_ffn_weights2, L1_ffn_bias2)
    return x

_drawn_inputs = setup_inputs


def setup_inputs(seed=0):
    import zlib

    import numpy as np

    out = dict(_drawn_inputs(seed))
    spreads = {}
    factors = {'fside_Bx1x1024x16_0': 2.842,
     'L0_ffn_b1': 8.0,
     'L0_ffn_b2': 8.0,
     'L1_cond_Wxz': 8.0,
     'L1_cond_bxz': 8.0,
     'L1_cond_Whz': 8.0,
     'L1_cond_bhz': 8.0,
     'L1_cond_Wxr': 8.0,
     'L1_cond_bxr': 184.841,
     'L1_cond_Whr': 24.315,
     'L1_cond_bhr': 200.0,
     'L1_cond_Wxh': 8.0,
     'L1_cond_bxh': 8.0,
     'L1_cond_Whh': 8.0,
     'L1_cond_bhh': 8.0,
     'L1_cond_Whq': 8.0,
     'L1_cond_bhq': 8.0,
     'L1_ffn_router_w': 8.0,
     'L1_ffn_router_b': 8.0,
     'L1_ffn_weights1': 8.0,
     'L1_ffn_bias1': 54.938,
     'L1_ffn_weights2': 8.0,
     'L1_ffn_bias2': 182.352}
    for name, (base, spread) in spreads.items():
        noise = np.random.default_rng([zlib.crc32(name.encode()), seed]).standard_normal(out[name].shape)
        drawn = base * np.exp(spread * noise) if base else spread * noise
        out[name] = jnp.asarray(drawn.astype(out[name].dtype))
    for name, factor in factors.items():
        out[name] = (out[name] * factor).astype(out[name].dtype)
    return out
```

```python
from contextlib import ExitStack

import numpy as np

import concourse.bass as bass
from concourse import mybir

F32 = mybir.dt.float32
BF16 = mybir.dt.bfloat16
U32 = mybir.dt.uint32
ALU = mybir.AluOpType
ACT = mybir.ActivationFunctionType
AX = mybir.AxisListType

B, T, C = 16, 128, 128
R = 16
FF = 4 * C
NF = FF // C
E, HE = 32, 32
NE = E * HE // 128
STEPS = 16
K = T // STEPS
N = STEPS * B
EPS = 1e-5
LOW_RANK_SCALE = 1.0 / (C * R)
OFF = 1e30

V_FC, V_COND, V_B1, V_B2, V_BHQ, V_E1 = 0, 1, 1 + B, 1 + B + NF, 2 + B + NF, 3 + B + NF
NV = V_E1 + NE
WXR, WXZ, WXH, WHR, WHZ, WHH, WHQ = range(7)
GATES = 3


def cols(k, n=N):
    return slice(k * n, (k + 1) * n) if isinstance(k, int) else bass.ds(k * n, n)


def build(nc, xT, vT, early, vectors, ffn, gru, gate_bias, consts, expand, router,
          w1, w2, bias2, outT):
    ctx = ExitStack()
    with ctx:
        def sb(name, shape, dt=F32):
            return ctx.enter_context(nc.sbuf_tensor(name, shape, dt))

        def bank(name):
            return ctx.enter_context(nc.psum_tensor(name, [128, 512], F32))

        def sem(name):
            return ctx.enter_context(nc.semaphore(name))

        x_sb = sb("x_sb", [128, B, T])
        v_sb = sb("v_sb", [R, B, C])
        wt_sb = sb("wt_sb", [128, C])
        vec = sb("vec", [128, NV])
        ffn_sb = sb("ffn_sb", [128, 2, FF])
        gru_sb = sb("gru_sb", [128, 7, C])
        gb_sb = sb("gb_sb", [3, 2, GATES, C])
        const_sb = sb("const_sb", [128, 128 + 96 + 3])
        expand_sb = sb("expand_sb", [E, NE * 128])
        router_sb = sb("router_sb", [128, 2, E])
        w1_sb = sb("w1_sb", [128, NE * 128])
        w2_sb = sb("w2_sb", [128, NE, C])
        b2_sb = sb("b2_sb", [96, C])

        weff = sb("weff", [128, B, C])
        seq_bias = sb("seq_bias", [128, B])
        pre = sb("pre", [128, 2, 4, T])
        g = sb("g", [128, T * B])
        ones = sb("ones", [128, 128])
        ones3 = sb("ones3", [3, N], BF16)
        asum = sb("asum", [128, 2])
        gam = sb("gam", [128, 2])
        thr = sb("thr", [128, 2])
        nthr = sb("nthr", [128, 2])
        below = sb("below", [128, 2, FF])
        wq = sb("wq", [128, 2, FF])
        gsum = sb("gsum", [3, GATES * C])
        gres = sb("gres", [3, 2, GATES * C])
        gpart = sb("gpart", [3, 3, GATES * C], BF16)
        gpick = sb("gpick", [3, 2, GATES * C], BF16)
        gbias3 = sb("gbias3", [3, GATES * C], BF16)
        ident = sb("ident", [128, 128], BF16)
        expand_off = sb("expand_off", [E, NE * 128], BF16)
        b2res = sb("b2res", [96, 2, C])
        b2part = sb("b2part", [96, 3, C], BF16)
        b2pick = sb("b2pick", [96, 2, C], BF16)
        bias2_3 = sb("bias2_3", [96, C], BF16)

        x1 = sb("x1", [128, T * B])
        hid = sb("hid", [128, 4, N])
        hist = sb("hist", [128, 2, N])
        y_sb = sb("y_sb", [128, N])
        lg = sb("lg", [128, 2, E])
        top = sb("top", [128, 2, 8])
        idx = sb("idx", [128, 2, 8], U32)
        pen = sb("pen", [128, 2, 96], BF16)
        penT = sb("penT", [E, N], BF16)
        maskT = sb("maskT", [96, N], BF16)
        res = sb("res", [128, 2, N])

        r_sb = sb("r_sb", [128, 2, B])
        z_sb = sb("z_sb", [128, 2, B])
        cand = sb("cand", [128, 2, B])
        keep = sb("keep", [128, 2, B])
        rh = sb("rh", [128, 2, B])
        zh = sb("zh", [128, 2, B])
        m = sb("m", [128, 2, B])

        R_bank = [bank("R0"), bank("R1")]
        ZH_bank = [bank("ZH0"), bank("ZH1")]
        F_bank = [bank("F0"), bank("F1")]
        O_bank = bank("O")
        L_bank = bank("L")
        maskT_ps = L_bank[:, 320:320 + N // 2].bitcast(BF16)

        x_in = [sem(f"x_in{i}") for i in range(4)]
        v_in, early_in, vec_in, ffn_in, gru_in = (sem(n) for n in
            ("v_in", "early_in", "vec_in", "ffn_in", "gru_in"))
        gb_in, const_in, expand_in, router_in, w1_in, w2_in, b2_in = (sem(n) for n in
            ("gb_in", "const_in", "expand_in", "router_in", "w1_in", "w2_in", "b2_in"))
        ones_set = sem("ones_set")
        vv_mm, weff_made, pre_mm, pre_made, g_made = (sem(n) for n in
            ("vv_mm", "weff_made", "pre_mm", "pre_made", "g_made"))
        bias_made, asum_made, gamma_mm, thr_step, below_made, wq_made = (sem(n) for n in
            ("bias_made", "asum_made", "gamma_mm", "thr_step", "below_made", "wq_made"))
        gb_step, b2_step, ident_made, expand_made = (sem(n) for n in
            ("gb_step", "b2_step", "ident_made", "expand_made"))
        ffn_hid_mm, ffn_relu, ffn_out_mm, x1_made = (sem(n) for n in
            ("ffn_hid_mm", "ffn_relu", "ffn_out_mm", "x1_made"))
        proj_mm = sem("proj_mm")
        whq_mm, y2_made, logit_mm, logits_made, top_made, idx_made, pen_made = (sem(n) for n in
            ("whq_mm", "y2_made", "logit_mm", "logits_made", "top_made", "idx_made", "pen_made"))
        turn_mm, masks_made, exp_hid_mm, exp_relu, exp_out_mm, res_made, out_sent = (sem(n) for n in
            ("turn_mm", "masks_made", "exp_hid_mm", "exp_relu", "exp_out_mm", "res_made", "out_sent"))
        r_mm, z_mm, cand_mm = sem("r_mm"), sem("z_mm"), sem("cand_mm")
        r_made, z_made, cand_made = sem("r_made"), sem("z_made"), sem("cand_made")
        rh_made, zh_made, keep_made, m_made, h_made = (sem(n) for n in
            ("rh_made", "zh_made", "keep_made", "m_made", "h_made"))

        block = ctx.enter_context(nc.Block())

        def hist_col(par, t):
            if t < 0:
                par, t = 1 - par, STEPS - 1
            return hist[:, par, t * B:(t + 1) * B]

        @block.sync
        def _(sp):
            sp.dma_start(v_sb[:], vT).then_inc(v_in, 16)
            for i in range(4):
                sp.dma_start(x_sb[:, 4 * i:4 * i + 4, :], xT[:, 4 * i:4 * i + 4, :]).then_inc(x_in[i], 16)
            sp.dma_start(gb_sb[:], gate_bias).then_inc(gb_in, 16)
            sp.dma_start(const_sb[:], consts).then_inc(const_in, 16)
            sp.dma_start(router_sb[:], router).then_inc(router_in, 16)
            sp.dma_start(w2_sb[:], w2).then_inc(w2_in, 16)
            sp.dma_start(b2_sb[:], bias2).then_inc(b2_in, 16)

            def store(f, par):
                sp.wait_ge(res_made, f + 1)
                sp.dma_start(outT[:, cols(f)], res[:, par, :]).then_inc(out_sent, 16)
                sp.wait_ge(out_sent, 16 * f + 16)

            for f in range(K):
                store(f, f % 2)

        @block.gpsimd
        def _(pool):
            nc.gpsimd.memset(ones[:], 1.0).then_inc(ones_set, 1)
            nc.gpsimd.memset(ones3[:], 1.0).then_inc(ones_set, 1)

        @block.scalar
        def _(act):
            act.dma_start(wt_sb[:], early).then_inc(early_in, 16)
            act.dma_start(vec[:], vectors).then_inc(vec_in, 16)
            act.dma_start(ffn_sb[:], ffn).then_inc(ffn_in, 16)
            act.dma_start(gru_sb[:], gru).then_inc(gru_in, 16)
            act.dma_start(expand_sb[:], expand).then_inc(expand_in, 16)
            act.dma_start(w1_sb[:], w1).then_inc(w1_in, 16)

            def ffn_hidden_relu(n, j):
                act.wait_ge(ffn_hid_mm, n * NF + j + 1)
                nc.scalar.activation(hid[:, j, :], F_bank[j % 2][:, 0:N], ACT.Relu,
                                     bias=vec[:, V_B1 + j:V_B1 + j + 1]).then_inc(ffn_relu, 1)

            def y_evacuate(q):
                act.wait_ge(whq_mm, q + 1)
                nc.scalar.activation(y_sb[:], L_bank[:, 0:N], ACT.Identity,
                                     bias=vec[:, V_BHQ:V_BHQ + 1]).then_inc(y2_made, 1)

            def expert_relu(q, c):
                act.wait_ge(exp_hid_mm, q * NE + c + 1)
                nc.scalar.activation(hid[:, c % 4, :], F_bank[c % 2][:, 0:N], ACT.Relu,
                                     bias=vec[:, V_E1 + c:V_E1 + c + 1]).then_inc(exp_relu, 1)

            for i in range(4):
                act.wait_ge(pre_made, i + 1)
                nc.scalar.activation(g[:].rearrange("p (t b) -> p b t", b=B)[:, 4 * i:4 * i + 4, :],
                                     pre[:, i % 2, :, :], ACT.Gelu).then_inc(g_made, 1)
            for j in range(NF):
                ffn_hidden_relu(0, j)

            def gru_chunk(k, par, experts, ffn):
                for t in range(STEPS):
                    p = t % 2
                    act.wait_ge(r_mm, k * STEPS + t + 1)
                    nc.scalar.activation(r_sb[:, p, :], R_bank[par][:, t * B:(t + 1) * B],
                                         ACT.Sigmoid).then_inc(r_made, 1)
                    act.wait_ge(z_mm, k * STEPS + t + 1)
                    nc.scalar.activation(z_sb[:, p, :], ZH_bank[par][:, t * B:(t + 1) * B],
                                         ACT.Sigmoid).then_inc(z_made, 1)
                    if experts and t == 1:
                        y_evacuate(k - 1)
                    act.wait_ge(cand_mm, k * STEPS + t + 1)
                    nc.scalar.activation(cand[:, p, :], ZH_bank[par][:, N + t * B:N + (t + 1) * B],
                                         ACT.Tanh).then_inc(cand_made, 1)
                    if ffn and t < NF:
                        ffn_hidden_relu(k + 1, t)
                    if experts and 7 <= t < 7 + NE:
                        expert_relu(k - 1, t - 7)

            gru_chunk(0, 0, False, True)
            for k in range(1, K - 1):
                gru_chunk(k, k % 2, True, True)
            gru_chunk(K - 1, (K - 1) % 2, True, False)
            y_evacuate(K - 1)
            for c in range(NE):
                expert_relu(K - 1, c)

        @block.vector
        def _(dve):
            def x1_evacuate(n):
                dve.wait_ge(ffn_out_mm, n + 1)
                nc.vector.scalar_tensor_tensor(
                    out=x1[:, cols(n)].rearrange("p (t b) -> p t b", b=B),
                    in0=O_bank[:, 0:N].rearrange("p (t b) -> p t b", b=B),
                    scalar=vec[:, V_B2:V_B2 + 1],
                    in1=x_sb[:, :, cols(n, STEPS)].rearrange("p b t -> p t b"),
                    op0=ALU.add, op1=ALU.add).then_inc(x1_made, 1)

            def logits(q):
                dve.wait_ge(logit_mm, q + 1)
                nc.vector.tensor_tensor(
                    lg[:], L_bank[:, N:N + 2 * E].rearrange("p (i e) -> p i e", i=2),
                    router_sb[:, 1:2, :].broadcast_to([128, 2, E]), ALU.add).then_inc(logits_made, 1)

            def best_logit(q):
                dve.wait_ge(logits_made, q + 1)
                for i in range(2):
                    nc.vector.max(top[:, i, :], lg[:, i, :]).then_inc(top_made, 1)

            def best_expert(q):
                dve.wait_ge(top_made, 2 * q + 2)
                for i in range(2):
                    nc.vector.max_index(idx[:, i, :], top[:, i, :], lg[:, i, :]).then_inc(idx_made, 1)

            def penalties(q):
                dve.wait_ge(idx_made, 2 * q + 2)
                for i in range(2):
                    nc.vector.tensor_scalar(pen[:, i, :], const_sb[:, 128:224], idx[:, i, 0:1], 1.0,
                                            ALU.is_equal, ALU.subtract).then_inc(pen_made, 1)

            def masks(q):
                dve.wait_ge(turn_mm, q + 1)
                nc.vector.tensor_copy(penT[:], maskT_ps[0:E, :]).then_inc(masks_made, 1)
                nc.vector.tensor_scalar(maskT[:], maskT_ps[0:96, :], 1.0, None, ALU.add).then_inc(masks_made, 1)

            def finish(f, par):
                dve.wait_ge(exp_out_mm, f * NE + NE)
                if not isinstance(f, int) or f >= 2:
                    dve.wait_ge(out_sent, f * 16 - 16)
                nc.vector.scalar_tensor_tensor(out=res[:, par, :], in0=O_bank[:, 0:N], scalar=0.0,
                                               in1=x1[:, cols(f)], op0=ALU.max,
                                               op1=ALU.add).then_inc(res_made, 1)

            dve.wait_ge(vec_in, 16)
            nc.vector.tensor_scalar(seq_bias[:], vec[:, V_COND:V_COND + B], vec[:, V_FC:V_FC + 1], None,
                                    ALU.add).then_inc(bias_made, 1)
            nc.vector.tensor_copy(hist[:, 1, (STEPS - 1) * B:N], vec[:, V_COND:V_COND + B]).then_inc(h_made, 1)
            dve.wait_ge(early_in, 16)
            for i in range(4):
                dve.wait_ge(vv_mm, i + 1)
                nc.vector.scalar_tensor_tensor(
                    out=weff[:, 4 * i:4 * i + 4, :],
                    in0=[F_bank[0], F_bank[1], R_bank[0], R_bank[1]][i][:].rearrange("p (b c) -> p b c", b=4),
                    scalar=LOW_RANK_SCALE,
                    in1=wt_sb[:].rearrange("p (o c) -> p o c", o=1).broadcast_to([128, 4, C]),
                    op0=ALU.mult, op1=ALU.add).then_inc(weff_made, 1)
            dve.wait_ge(ffn_in, 16)
            nc.vector.tensor_reduce(asum[:], ffn_sb[:], AX.X, ALU.add,
                                    apply_absolute_value=True).then_inc(asum_made, 1)
            dve.wait_ge(bias_made, 1)
            for i in range(4):
                dve.wait_ge(pre_mm, i + 1)
                if i >= 2:
                    dve.wait_ge(g_made, i - 1)
                nc.vector.tensor_tensor(
                    pre[:, i % 2, :, :],
                    [ZH_bank[0], ZH_bank[1], O_bank, L_bank][i][:].rearrange("p (b t) -> p b t", b=4),
                    seq_bias[:, 4 * i:4 * i + 4].rearrange("p (b o) -> p b o", o=1).broadcast_to([128, 4, T]),
                    ALU.add).then_inc(pre_made, 1)
                if i == 0:
                    dve.wait_ge(gamma_mm, 1)
                    nc.vector.tensor_scalar(gam[:], F_bank[0][:, 0:2], 1.0 / (FF * C), EPS,
                                            ALU.mult, ALU.add).then_inc(thr_step, 1)
                    dve.wait_ge(thr_step, 1)
                    nc.vector.tensor_scalar(thr[:], gam[:], 0.5, None, ALU.mult).then_inc(thr_step, 1)
                    nc.vector.tensor_scalar(nthr[:], gam[:], -0.5, None, ALU.mult).then_inc(thr_step, 1)
                    dve.wait_ge(thr_step, 3)
                if i < 2:
                    nc.vector.tensor_scalar(below[:, i, :], ffn_sb[:, i, :], nthr[:, i:i + 1], None,
                                            ALU.is_lt).then_inc(below_made, 1)
                else:
                    dve.wait_ge(below_made, i - 1)
                    nc.vector.scalar_tensor_tensor(out=wq[:, i - 2, :], in0=ffn_sb[:, i - 2, :],
                                                   scalar=thr[:, i - 2:i - 1], in1=below[:, i - 2, :],
                                                   op0=ALU.is_gt, op1=ALU.subtract).then_inc(wq_made, 1)
            dve.wait_ge(gb_in, 16)
            dve.wait_ge(const_in, 16)
            flat = gb_sb[:].rearrange("p s g c -> p s (g c)")
            nc.vector.tensor_tensor(gsum[:], flat[:, 0, :], flat[:, 1, :], ALU.add).then_inc(gb_step, 1)
            dve.wait_ge(gb_step, 1)
            nc.vector.tensor_copy(gpart[:, 0, :], gsum[:]).then_inc(gb_step, 1)
            dve.wait_ge(gb_step, 2)
            nc.vector.tensor_tensor(gres[:, 0, :], gsum[:], gpart[:, 0, :], ALU.subtract).then_inc(gb_step, 1)
            dve.wait_ge(gb_step, 3)
            nc.vector.tensor_copy(gpart[:, 1, :], gres[:, 0, :]).then_inc(gb_step, 1)
            dve.wait_ge(gb_step, 4)
            nc.vector.tensor_tensor(gres[:, 1, :], gres[:, 0, :], gpart[:, 1, :], ALU.subtract).then_inc(gb_step, 1)
            dve.wait_ge(gb_step, 5)
            nc.vector.tensor_copy(gpart[:, 2, :], gres[:, 1, :]).then_inc(gb_step, 1)
            pick = const_sb[:, 224:227]
            nc.vector.tensor_scalar(gpick[:, 0, :], gpart[:, 0, :], pick[0:3, 0:1], None, ALU.mult).then_inc(gb_step, 1)
            dve.wait_ge(gb_step, 7)
            nc.vector.scalar_tensor_tensor(out=gpick[:, 1, :], in0=gpart[:, 1, :], scalar=pick[0:3, 1:2],
                                           in1=gpick[:, 0, :], op0=ALU.mult, op1=ALU.add).then_inc(gb_step, 1)
            dve.wait_ge(gb_step, 8)
            nc.vector.scalar_tensor_tensor(out=gbias3[:], in0=gpart[:, 2, :], scalar=pick[0:3, 2:3],
                                           in1=gpick[:, 1, :], op0=ALU.mult, op1=ALU.add).then_inc(gb_step, 1)
            x1_evacuate(0)

            def router_constants(t):
                if t == 1:
                    nc.vector.tensor_copy(ident[:], const_sb[:, 0:128]).then_inc(ident_made, 1)
                if t == 2:
                    dve.wait_ge(expand_in, 16)
                    nc.vector.tensor_scalar(expand_off[:], expand_sb[:], OFF, None, ALU.mult).then_inc(expand_made, 1)
                if t == 6:
                    dve.wait_ge(b2_in, 16)
                    nc.vector.tensor_copy(b2part[:, 0, :], b2_sb[:]).then_inc(b2_step, 1)
                if t == 7:
                    dve.wait_ge(b2_step, 1)
                    nc.vector.tensor_tensor(b2res[:, 0, :], b2_sb[:], b2part[:, 0, :], ALU.subtract).then_inc(b2_step, 1)
                if t == 8:
                    dve.wait_ge(b2_step, 2)
                    nc.vector.tensor_copy(b2part[:, 1, :], b2res[:, 0, :]).then_inc(b2_step, 1)
                if t == 9:
                    dve.wait_ge(b2_step, 3)
                    nc.vector.tensor_tensor(b2res[:, 1, :], b2res[:, 0, :], b2part[:, 1, :], ALU.subtract).then_inc(b2_step, 1)
                if t == 10:
                    dve.wait_ge(b2_step, 4)
                    nc.vector.tensor_copy(b2part[:, 2, :], b2res[:, 1, :]).then_inc(b2_step, 1)
                if t == 11:
                    dve.wait_ge(b2_step, 5)
                    for i in range(3):
                        rows = slice(32 * i, 32 * i + 32)
                        nc.vector.tensor_copy(bias2_3[rows, :], b2part[rows, i, :]).then_inc(b2_step, 1)

            def gru_chunk(k, par, first, experts, ffn, fin):
                for t in range(STEPS):
                    p, q = t % 2, (t + 1) % 2
                    h_old, h_new = hist_col(par, t - 1), hist_col(par, t)
                    step = k * STEPS + t
                    dve.wait_ge(h_made, step + 1)
                    dve.wait_ge(r_made, step + 1)
                    nc.vector.tensor_tensor(rh[:, p, :], r_sb[:, p, :], h_old, ALU.mult).then_inc(rh_made, 1)
                    dve.wait_ge(z_made, step + 1)
                    nc.vector.tensor_tensor(zh[:, q, :], z_sb[:, p, :], h_old, ALU.mult).then_inc(zh_made, 1)
                    nc.vector.tensor_scalar(keep[:, p, :], z_sb[:, p, :], -1.0, 1.0,
                                            ALU.mult, ALU.add).then_inc(keep_made, 1)
                    dve.wait_ge(keep_made, step + 1)
                    dve.wait_ge(cand_made, step + 1)
                    nc.vector.tensor_tensor(m[:, q, :], keep[:, p, :], cand[:, p, :], ALU.mult).then_inc(m_made, 1)
                    dve.wait_ge(m_made, step + 1)
                    nc.vector.tensor_tensor(h_new, zh[:, q, :], m[:, q, :], ALU.add).then_inc(h_made, 1)
                    if first:
                        router_constants(t)
                    if fin and t == 0:
                        finish(k - 2, par)
                    if experts:
                        if t == 2:
                            logits(k - 1)
                        if t == 3:
                            best_logit(k - 1)
                        if t == 4:
                            best_expert(k - 1)
                        if t == 5:
                            penalties(k - 1)
                        if t == 6:
                            masks(k - 1)
                    if ffn and t == 5:
                        x1_evacuate(k + 1)

            dve.wait_ge(router_in, 16)
            gru_chunk(0, 0, True, False, True, False)
            gru_chunk(1, 1, False, True, True, False)
            for k in range(2, K - 1):
                gru_chunk(k, k % 2, False, True, True, True)
            gru_chunk(K - 1, (K - 1) % 2, False, True, False, True)
            finish(K - 2, K % 2)
            logits(K - 1)
            best_logit(K - 1)
            best_expert(K - 1)
            penalties(K - 1)
            masks(K - 1)
            finish(K - 1, (K - 1) % 2)

        @block.tensor
        def _(pe):
            mm = nc.tensor.matmul

            def ffn_hidden(n, j):
                if j >= 2:
                    pe.wait_ge(ffn_relu, n * NF + j - 1)
                mm(F_bank[j % 2][:, 0:N], wq[:, 0, j * 128:(j + 1) * 128], g[:, cols(n)],
                   start=True, stop=True).then_inc(ffn_hid_mm, 1)

            def ffn_out(n, j):
                pe.wait_ge(ffn_relu, n * NF + j + 1)
                i = mm(O_bank[:, 0:N], wq[:, 1, j * 128:(j + 1) * 128], hid[:, j, :],
                       start=(j == 0), stop=(j == NF - 1))
                if j == NF - 1:
                    i.then_inc(ffn_out_mm, 1)

            def project(n, par, gate):
                out = [R_bank[par][:, 0:N], ZH_bank[par][:, 0:N], ZH_bank[par][:, N:2 * N]][gate]
                if gate == 0:
                    pe.wait_ge(x1_made, n + 1)
                mm(out, gbias3[:, gate * C:(gate + 1) * C], ones3[:], start=(gate < 2), stop=False,
                   skip_group_check=True)
                mm(out, gru_sb[:, WXR + gate, :], x1[:, cols(n)], start=False, stop=False,
                   skip_group_check=True)

            def whq(q, par):
                mm(L_bank[:, 0:N], gru_sb[:, WHQ, :], hist[:, par, :], start=True, stop=True).then_inc(whq_mm, 1)

            def router_logits(q):
                pe.wait_ge(y2_made, q + 1)
                for i in range(2):
                    ins = mm(L_bank[:, N + i * E:N + (i + 1) * E], y_sb[:, i * 128:(i + 1) * 128],
                             router_sb[:, 0, :], start=True, stop=True)
                ins.then_inc(logit_mm, 1)

            def turn_masks(q):
                pe.wait_ge(pen_made, 2 * q + 2)
                for i in range(2):
                    ins = nc.tensor.transpose(maskT_ps[0:96, i * 128:(i + 1) * 128], pen[:, i, :], ident[:])
                ins.then_inc(turn_mm, 1)

            def expert_hidden(q, c):
                if c == 0:
                    pe.wait_ge(masks_made, 2 * q + 2)
                if c >= 2:
                    pe.wait_ge(exp_relu, q * NE + c - 1)
                mm(F_bank[c % 2][:, 0:N], expand_off[:, c * 128:(c + 1) * 128], penT[:], start=True, stop=False)
                mm(F_bank[c % 2][:, 0:N], w1_sb[:, c * 128:(c + 1) * 128], y_sb[:],
                   start=False, stop=True).then_inc(exp_hid_mm, 1)

            def expert_out(q, c):
                pe.wait_ge(exp_relu, q * NE + c + 1)
                if c == 0:
                    mm(O_bank[:, 0:N], bias2_3[:], maskT[:], start=True, stop=False)
                mm(O_bank[:, 0:N], w2_sb[:, c, :], hid[:, c % 4, :],
                   start=False, stop=(c == NE - 1)).then_inc(exp_out_mm, 1)

            pe.wait_ge(v_in, 16)
            for i in range(4):
                for b in range(4 * i, 4 * i + 4):
                    ins = mm([F_bank[0], F_bank[1], R_bank[0], R_bank[1]][i][:, (b % 4) * C:(b % 4 + 1) * C],
                             v_sb[:, b, :], v_sb[:, b, :], start=True, stop=True)
                ins.then_inc(vv_mm, 1)
            for i in range(4):
                pe.wait_ge(weff_made, i + 1)
                pe.wait_ge(x_in[i], 16)
                for b in range(4 * i, 4 * i + 4):
                    ins = mm([ZH_bank[0], ZH_bank[1], O_bank, L_bank][i][:, (b % 4) * T:(b % 4 + 1) * T],
                             weff[:, b, :], x_sb[:, b, :], start=True, stop=True)
                ins.then_inc(pre_mm, 1)
                if i == 0:
                    pe.wait_ge(asum_made, 1)
                    pe.wait_ge(ones_set, 2)
                    mm(F_bank[0][:, 0:2], ones[:], asum[:], start=True, stop=True).then_inc(gamma_mm, 1)
            pe.wait_ge(g_made, 4)
            pe.wait_ge(wq_made, 2)
            pe.wait_ge(gru_in, 16)
            ffn_hidden(0, 0)
            ffn_hidden(0, 1)
            ffn_out(0, 0)
            ffn_hidden(0, 2)
            ffn_out(0, 1)
            ffn_hidden(0, 3)
            ffn_out(0, 2)
            ffn_out(0, 3)
            pe.wait_ge(gb_step, 9)
            for gate in range(GATES):
                project(0, 0, gate)

            def gru_chunk(k, par, first, experts, ffn, fin):
                for t in range(STEPS):
                    q = t % 2
                    step = k * STEPS + t
                    at = slice(t * B, (t + 1) * B)
                    h_old = hist_col(par, t - 1)
                    if first and t == 0:
                        pe.wait_ge(h_made, 1)
                        mm(R_bank[par][:, at], gru_sb[:, WHR, :], h_old, start=False, stop=True,
                           skip_group_check=True).then_inc(r_mm, 1)
                    else:
                        pe.wait_ge(zh_made, step)
                        mm(R_bank[par][:, at], gru_sb[:, WHR, :], zh[:, q, :], start=False, stop=False,
                           skip_group_check=True)
                        pe.wait_ge(m_made, step)
                        mm(R_bank[par][:, at], gru_sb[:, WHR, :], m[:, q, :], start=False, stop=True,
                           skip_group_check=True).then_inc(r_mm, 1)
                    pe.wait_ge(h_made, step + 1)
                    mm(ZH_bank[par][:, at], gru_sb[:, WHZ, :], h_old, start=False, stop=True,
                       skip_group_check=True).then_inc(z_mm, 1)
                    if ffn and t < NF:
                        ffn_hidden(k + 1, t)
                    if ffn and t == 5:
                        ffn_out(k + 1, 3)
                    if experts and t == 6:
                        turn_masks(k - 1)
                    if experts and 7 <= t < 7 + NE:
                        expert_hidden(k - 1, t - 7)
                    if ffn and t == 15:
                        project(k + 1, 1 - par, 2)
                    pe.wait_ge(z_made, step + 1)
                    pe.wait_ge(rh_made, step + 1)
                    mm(ZH_bank[par][:, N + t * B:N + (t + 1) * B], gru_sb[:, WHH, :], rh[:, q, :],
                       start=False, stop=True, skip_group_check=True).then_inc(cand_mm, 1)
                    if experts and t == 0:
                        whq(k - 1, 1 - par)
                    if experts and t == 1:
                        router_logits(k - 1)
                    if fin and t == 2:
                        pe.wait_ge(res_made, k - 1)
                    if ffn and 2 <= t < 5:
                        ffn_out(k + 1, t - 2)
                    if ffn and t == 6:
                        project(k + 1, 1 - par, 0)
                    if ffn and t == 7:
                        project(k + 1, 1 - par, 1)
                    if experts and 8 <= t < 8 + NE:
                        expert_out(k - 1, t - 8)

            gru_chunk(0, 0, True, False, True, False)
            for s, n in ((router_in, 16), (ident_made, 1), (expand_made, 1), (w1_in, 16), (w2_in, 16), (b2_step, 8)):
                pe.wait_ge(s, n)
            gru_chunk(1, 1, False, True, True, False)
            for k in range(2, K - 1):
                gru_chunk(k, k % 2, False, True, True, True)
            gru_chunk(K - 1, (K - 1) % 2, False, True, False, True)
            pe.wait_ge(h_made, K * STEPS + 1)
            whq(K - 1, (K - 1) % 2)
            router_logits(K - 1)
            turn_masks(K - 1)
            expert_hidden(K - 1, 0)
            expert_hidden(K - 1, 1)
            pe.wait_ge(res_made, K - 1)
            for c in range(NE):
                expert_out(K - 1, c)
                if c + 2 < NE:
                    expert_hidden(K - 1, c + 2)


def kernel(x, fside_Bx1x1024x16_0, cond_1024, L0_cond_W, L0_cond_fc_bias, L0_ffn_W1, L0_ffn_b1,
           L0_ffn_W2, L0_ffn_b2, L1_cond_Wxz, L1_cond_bxz, L1_cond_Whz, L1_cond_bhz, L1_cond_Wxr,
           L1_cond_bxr, L1_cond_Whr, L1_cond_bhr, L1_cond_Wxh, L1_cond_bxh, L1_cond_Whh, L1_cond_bhh,
           L1_cond_Whq, L1_cond_bhq, L1_ffn_router_w, L1_ffn_router_b, L1_ffn_weights1,
           L1_ffn_bias1, L1_ffn_weights2, L1_ffn_bias2):
    import concourse.bacc as bacc
    from concourse.bass_utils import run_bass_kernel_spmd

    a = np.asarray
    f32 = np.float32
    rows = [a(L0_cond_fc_bias)[None], a(cond_1024), a(L0_ffn_b1).reshape(NF, 128), a(L0_ffn_b2)[None],
            a(L1_cond_bhq)[None], a(L1_ffn_bias1).reshape(NE, 128)]
    arrays = {
        "xT": a(x).transpose(2, 0, 1),
        "vT": a(fside_Bx1x1024x16_0)[:, 0].transpose(2, 0, 1),
        "early": a(L0_cond_W).T,
        "vectors": np.concatenate(rows, 0).T,
        "ffn": np.stack([a(L0_ffn_W1).T, a(L0_ffn_W2).T.reshape(NF, 128, C).transpose(1, 0, 2).reshape(128, FF)], 1),
        "gru": np.stack([a(w).T for w in (L1_cond_Wxr, L1_cond_Wxz, L1_cond_Wxh, L1_cond_Whr,
                                          L1_cond_Whz, L1_cond_Whh, L1_cond_Whq)], 1),
        "gate_bias": np.stack([np.stack([np.stack([a(L1_cond_bxr), a(L1_cond_bxz), a(L1_cond_bxh)]),
                                         np.stack([a(L1_cond_bhr), a(L1_cond_bhz), a(L1_cond_bhh)])])] * 3),
        "consts": np.concatenate([np.eye(128, dtype=f32), np.tile(np.arange(E, dtype=f32), (128, 3)),
                                  np.eye(128, 3, dtype=f32)], 1),
        "expand": np.repeat(np.eye(E, dtype=f32), HE, axis=1),
        "router": np.stack([a(L1_ffn_router_w).T, np.stack([a(L1_ffn_router_b)] * 128)], 1),
        "w1": a(L1_ffn_weights1).transpose(1, 0, 2).reshape(C, E * HE),
        "w2": a(L1_ffn_weights2).reshape(NE, 128, C).transpose(1, 0, 2),
        "bias2": np.concatenate([a(L1_ffn_bias2)] * 3, 0),
    }
    arrays = {n: np.ascontiguousarray(v) for n, v in arrays.items()}

    nc = bacc.Bacc("TRN2", target_bir_lowering=False, num_devices=1)
    args = [nc.dram_tensor(n, v.shape, mybir.dt.from_np(v.dtype), kind="ExternalInput").ap()
            for n, v in arrays.items()]
    out = nc.dram_tensor("outT", (C, T * B), F32, kind="ExternalOutput").ap()
    build(nc, *args, out)
    r = run_bass_kernel_spmd(nc, [arrays], core_ids=[0])
    return np.ascontiguousarray(a(r.results[0]["outT"]).reshape(C, T, B).transpose(2, 1, 0))
```

```python
from contextlib import ExitStack

import numpy as np

import concourse.bass as bass
from concourse import mybir

F32 = mybir.dt.float32
BF16 = mybir.dt.bfloat16
F16 = mybir.dt.float16
U32 = mybir.dt.uint32
ALU = mybir.AluOpType
ACT = mybir.ActivationFunctionType
AX = mybir.AxisListType

B, T, C = 16, 128, 128
R = 16
FF = 4 * C
NF = FF // C
E, HE = 32, 32
NE = E * HE // 128
STEPS = 16
K = T // STEPS
N = STEPS * B
EPS = 1e-5
LOW_RANK_SCALE = 1.0 / (C * R)
OFF = 1e30

V_FC, V_COND, V_B1, V_B2, V_BHQ, V_E1 = 0, 1, 1 + B, 1 + B + NF, 2 + B + NF, 3 + B + NF
NV = V_E1 + NE
WXR, WXZ, WXH, WHR, WHZ, WHH, WHQ = range(7)
GATES = 3


def cols(k, n=N):
    return slice(k * n, (k + 1) * n) if isinstance(k, int) else bass.ds(k * n, n)


def build(nc, xT, vT, early, vectors, ffn, gru, gate_bias, consts, expand, router,
          w1, w2, bias2, outT):
    ctx = ExitStack()
    with ctx:
        def sb(name, shape, dt=F32):
            return ctx.enter_context(nc.sbuf_tensor(name, shape, dt))

        def bank(name):
            return ctx.enter_context(nc.psum_tensor(name, [128, 512], F32))

        def sem(name):
            return ctx.enter_context(nc.semaphore(name))

        x_sb = sb("x_sb", [128, B, T])
        v_sb = sb("v_sb", [R, B, C])
        wt_sb = sb("wt_sb", [128, C])
        vec = sb("vec", [128, NV])
        ffn_sb = sb("ffn_sb", [128, 2, FF])
        gru_sb = sb("gru_sb", [128, 7, C])
        gb_sb = sb("gb_sb", [3, 2, GATES, C])
        const_sb = sb("const_sb", [128, 128 + 96 + 3])
        expand_sb = sb("expand_sb", [E, NE * 128])
        router_sb = sb("router_sb", [128, 2, E])
        w1_sb = sb("w1_sb", [128, NE * 128])
        w2_sb = sb("w2_sb", [128, NE, C])
        b2_sb = sb("b2_sb", [96, C])

        weff = sb("weff", [128, B, C])
        seq_bias = sb("seq_bias", [128, B])
        pre = sb("pre", [128, 2, 4, T])
        g = sb("g", [128, T * B])
        g_hi = sb("g_hi", [128, T * B], F16)
        g_lo = sb("g_lo", [128, T * B], F16)
        ones = sb("ones", [128, 128])
        ones3 = sb("ones3", [3, N], BF16)
        asum = sb("asum", [128, 2])
        gam = sb("gam", [128, 2])
        thr = sb("thr", [128, 2])
        nthr = sb("nthr", [128, 2])
        below = sb("below", [128, 2, FF], F16)
        wq16 = sb("wq16", [128, 2, FF], F16)
        wq = sb("wq", [128, 2, FF])
        gsum = sb("gsum", [3, GATES * C])
        gres = sb("gres", [3, 2, GATES * C])
        gpart = sb("gpart", [3, 2, GATES * C], BF16)
        gpick = sb("gpick", [3, 4, GATES * C], BF16)
        gbias3 = sb("gbias3", [3, GATES * C], BF16)
        gru_hi = sb("gru_hi", [128, WHQ, C], F16)
        gru_lo = sb("gru_lo", [128, WHQ, C], F16)
        w1_hi = sb("w1_hi", [128, NE * 128], F16)
        w1_lo = sb("w1_lo", [128, NE * 128], F16)
        w2_hi = sb("w2_hi", [128, NE, C], F16)
        w2_lo = sb("w2_lo", [128, NE, C], F16)
        router_hi = sb("router_hi", [128, E], F16)
        router_lo = sb("router_lo", [128, E], F16)
        ident = sb("ident", [128, 128], BF16)
        expand_off = sb("expand_off", [E, NE * 128], BF16)
        b2res = sb("b2res", [96, 2, C])
        b2part = sb("b2part", [96, 3, C], BF16)
        b2pick = sb("b2pick", [96, 2, C], BF16)
        bias2_3 = sb("bias2_3", [96, C], BF16)

        x1 = sb("x1", [128, T * B])
        x1_hi = sb("x1_hi", [128, N], F16)
        x1_lo = sb("x1_lo", [128, N], F16)
        hid = sb("hid", [128, 2, N])
        hid_hi = sb("hid_hi", [128, 4, N], F16)
        hid_lo = sb("hid_lo", [128, 4, N], F16)
        hist = sb("hist", [128, 2, N])
        y_sb = sb("y_sb", [128, N])
        y_hi = sb("y_hi", [128, N], F16)
        y_lo = sb("y_lo", [128, N], F16)
        lg = sb("lg", [128, 2, E])
        top = sb("top", [128, 2, 8])
        idx = sb("idx", [128, 2, 8], U32)
        pen = sb("pen", [128, 2, 96], BF16)
        penT = sb("penT", [E, N], BF16)
        maskT = sb("maskT", [96, N], BF16)
        res = sb("res", [128, 2, N])

        r_sb = sb("r_sb", [128, 2, B])
        z_sb = sb("z_sb", [128, 2, B])
        cand = sb("cand", [128, 2, B])
        keep = sb("keep", [128, 2, B])
        rh = sb("rh", [128, 2, B])
        zh = sb("zh", [128, 2, B])
        m = sb("m", [128, 2, B])
        rh_p = sb("rh_p", [128, 2, 2, B], F16)
        zh_p = sb("zh_p", [128, 2, 2, B], F16)
        m_p = sb("m_p", [128, 2, 2, B], F16)

        R_bank = [bank("R0"), bank("R1")]
        ZH_bank = [bank("ZH0"), bank("ZH1")]
        F_bank = [bank("F0"), bank("F1")]
        O_bank = bank("O")
        L_bank = bank("L")
        vv_bank = [F_bank[0], F_bank[1], R_bank[0], R_bank[1]]
        pre_bank = [ZH_bank[0], ZH_bank[1], O_bank, L_bank]
        maskT_ps = L_bank[:, 320:320 + N // 2].bitcast(BF16)

        x_in = [sem(f"x_in{i}") for i in range(4)]
        v_in, early_in, vec_in, ffn_in, gru_in = (sem(n) for n in
            ("v_in", "early_in", "vec_in", "ffn_in", "gru_in"))
        gb_in, const_in, expand_in, router_in, w1_in, w2_in, b2_in = (sem(n) for n in
            ("gb_in", "const_in", "expand_in", "router_in", "w1_in", "w2_in", "b2_in"))
        ones_set = sem("ones_set")
        vv_mm, weff_made, pre_mm, pre_made, g_made = (sem(n) for n in
            ("vv_mm", "weff_made", "pre_mm", "pre_made", "g_made"))
        bias_made, asum_made, gamma_mm, thr_step, below_made, wq_made = (sem(n) for n in
            ("bias_made", "asum_made", "gamma_mm", "thr_step", "below_made", "wq_made"))
        gb_step, b2_step, ident_made, expand_made = (sem(n) for n in
            ("gb_step", "b2_step", "ident_made", "expand_made"))
        ffn_hid_mm, ffn_relu, ffn_out_mm, x1_made = (sem(n) for n in
            ("ffn_hid_mm", "ffn_relu", "ffn_out_mm", "x1_made"))
        proj_mm = sem("proj_mm")
        whq_mm, y2_made, logit_mm, logits_made, top_made, idx_made, pen_made = (sem(n) for n in
            ("whq_mm", "y2_made", "logit_mm", "logits_made", "top_made", "idx_made", "pen_made"))
        turn_mm, masks_made, exp_hid_mm, exp_relu, exp_out_mm, res_made, out_sent = (sem(n) for n in
            ("turn_mm", "masks_made", "exp_hid_mm", "exp_relu", "exp_out_mm", "res_made", "out_sent"))
        r_mm, z_mm, cand_mm = sem("r_mm"), sem("z_mm"), sem("cand_mm")
        r_made, z_made, cand_made = sem("r_made"), sem("z_made"), sem("cand_made")
        keep_made, h_made = sem("keep_made"), sem("h_made")
        rh_full, zh_full, m_full = sem("rh_full"), sem("zh_full"), sem("m_full")
        rh_hi, zh_hi, m_hi = sem("rh_hi"), sem("zh_hi"), sem("m_hi")
        rh_lo, zh_lo, m_lo = sem("rh_lo"), sem("zh_lo"), sem("m_lo")
        gru_hi_made, gru_lo_made = sem("gru_hi_made"), sem("gru_lo_made")
        wq16_made, ffn0_out = sem("wq16_made"), sem("ffn0_out")
        w1_hi_made, w2_hi_made, router_hi_made, w_lo_made = (sem(n) for n in
            ("w1_hi_made", "w2_hi_made", "router_hi_made", "w_lo_made"))
        g_hi_made, g_lo_made, x1_hi_made, x1_lo_made = (sem(n) for n in
            ("g_hi_made", "g_lo_made", "x1_hi_made", "x1_lo_made"))
        ffn_hi, ffn_lo, exp_hi, exp_lo, y_hi_made, y_lo_made = (sem(n) for n in
            ("ffn_hi", "ffn_lo", "exp_hi", "exp_lo", "y_hi_made", "y_lo_made"))

        block = ctx.enter_context(nc.Block())

        def hist_col(par, t):
            if t < 0:
                par, t = 1 - par, STEPS - 1
            return hist[:, par, t * B:(t + 1) * B]

        @block.sync
        def _(sp):
            sp.dma_start(v_sb[:], vT).then_inc(v_in, 16)
            for i in range(4):
                sp.dma_start(x_sb[:, 4 * i:4 * i + 4, :], xT[:, 4 * i:4 * i + 4, :]).then_inc(x_in[i], 16)
            sp.dma_start(router_sb[:], router).then_inc(router_in, 16)
            sp.dma_start(w2_sb[:], w2).then_inc(w2_in, 16)
            sp.dma_start(b2_sb[:], bias2).then_inc(b2_in, 16)

            def store(f, par):
                sp.wait_ge(res_made, f + 1)
                sp.dma_start(outT[:, cols(f)], res[:, par, :]).then_inc(out_sent, 16)
                sp.wait_ge(out_sent, 16 * f + 16)

            for f in range(K):
                store(f, f % 2)

        @block.gpsimd
        def _(pool):
            pool.dma_start(gb_sb[:], gate_bias).then_inc(gb_in, 16)
            pool.dma_start(const_sb[:], consts).then_inc(const_in, 16)
            nc.gpsimd.memset(ones[:], 1.0).then_inc(ones_set, 1)
            nc.gpsimd.memset(ones3[:], 1.0).then_inc(ones_set, 1)

            def g_low(n):
                pool.wait_ge(g_hi_made, n)
                nc.gpsimd.tensor_tensor(g_lo[:, cols(n)], g[:, cols(n)], g_hi[:, cols(n)],
                                        ALU.subtract).then_inc(g_lo_made, 1)

            def x1_low(n):
                pool.wait_ge(x1_hi_made, n)
                nc.gpsimd.tensor_tensor(x1_lo[:], x1[:, cols(n)], x1_hi[:], ALU.subtract).then_inc(x1_lo_made, 1)

            def ffn_low(n, j):
                pool.wait_ge(ffn_hi, (n - 1) * NF + j + 1)
                nc.gpsimd.tensor_tensor(hid_lo[:, j, :], hid[:, j % 2, :], hid_hi[:, j, :],
                                        ALU.subtract).then_inc(ffn_lo, 1)

            def y_low(q):
                pool.wait_ge(y_hi_made, q + 1)
                nc.gpsimd.tensor_tensor(y_lo[:], y_sb[:], y_hi[:], ALU.subtract).then_inc(y_lo_made, 1)

            def expert_low(q, c):
                pool.wait_ge(exp_hi, q * NE + c + 1)
                nc.gpsimd.tensor_tensor(hid_lo[:, c % 4, :], hid[:, c % 2, :], hid_hi[:, c % 4, :],
                                        ALU.subtract).then_inc(exp_lo, 1)

            pool.wait_ge(gb_in, 16)
            pool.wait_ge(const_in, 16)
            flat = gb_sb[:].rearrange("p s g c -> p s (g c)")
            pick = const_sb[:, 224:227]
            t_t, t_s = nc.gpsimd.tensor_tensor, nc.gpsimd.tensor_scalar
            t_t(gsum[:], flat[:, 0, :], flat[:, 1, :], ALU.add).then_inc(gb_step, 1)
            pool.wait_ge(gb_step, 1)
            t_s(gpart[:, 0, :], gsum[:], 0.0, None, ALU.add).then_inc(gb_step, 1)
            pool.wait_ge(gb_step, 2)
            t_t(gres[:, 0, :], gsum[:], gpart[:, 0, :], ALU.subtract).then_inc(gb_step, 1)
            pool.wait_ge(gb_step, 3)
            t_s(gpart[:, 1, :], gres[:, 0, :], 0.0, None, ALU.add).then_inc(gb_step, 1)
            pool.wait_ge(gb_step, 4)
            t_t(gres[:, 1, :], gres[:, 0, :], gpart[:, 1, :], ALU.subtract).then_inc(gb_step, 1)
            t_s(gpick[:, 0, :], gpart[:, 0, :], pick[0:3, 0:1], None, ALU.mult).then_inc(gb_step, 1)
            t_s(gpick[:, 1, :], gpart[:, 1, :], pick[0:3, 1:2], None, ALU.mult).then_inc(gb_step, 1)
            pool.wait_ge(gb_step, 7)
            t_s(gpick[:, 2, :], gres[:, 1, :], pick[0:3, 2:3], None, ALU.mult).then_inc(gb_step, 1)
            t_t(gpick[:, 3, :], gpick[:, 0, :], gpick[:, 1, :], ALU.add).then_inc(gb_step, 1)
            pool.wait_ge(gb_step, 9)
            t_t(gbias3[:], gpick[:, 2, :], gpick[:, 3, :], ALU.add).then_inc(gb_step, 1)
            g_low(1)

            def chunk(k, first, experts, ffn, more_g):
                if ffn:
                    ffn_low(k + 1, 0)
                if experts:
                    y_low(k - 1)
                if ffn:
                    for j in range(1, NF):
                        ffn_low(k + 1, j)
                    x1_low(k + 1)
                if more_g:
                    g_low(k + 2)
                if first:
                    for hi_made, full, hi, lo in ((w1_hi_made, w1_sb[:], w1_hi[:], w1_lo[:]),
                                                  (w2_hi_made, w2_sb[:], w2_hi[:], w2_lo[:]),
                                                  (router_hi_made, router_sb[:, 0, :], router_hi[:], router_lo[:])):
                        pool.wait_ge(hi_made, 1)
                        nc.gpsimd.tensor_tensor(lo, full, hi, ALU.subtract).then_inc(w_lo_made, 1)
                if experts:
                    for c in range(NE):
                        expert_low(k - 1, c)

            chunk(0, True, False, True, True)
            for k in range(1, K - 1):
                chunk(k, False, True, True, k + 2 < K)
            chunk(K - 1, False, True, False, False)
            y_low(K - 1)
            for c in range(NE):
                expert_low(K - 1, c)

        @block.scalar
        def _(act):
            act.dma_start(wt_sb[:], early).then_inc(early_in, 16)
            act.dma_start(vec[:], vectors).then_inc(vec_in, 16)
            act.dma_start(ffn_sb[:], ffn).then_inc(ffn_in, 16)
            act.dma_start(gru_sb[:], gru).then_inc(gru_in, 16)
            act.dma_start(expand_sb[:], expand).then_inc(expand_in, 16)
            act.dma_start(w1_sb[:], w1).then_inc(w1_in, 16)

            def ffn_hidden_relu(n, j):
                act.wait_ge(ffn_hid_mm, n * NF + j + 1)
                if j >= 2:
                    if isinstance(n, int) and n == 0:
                        act.wait_ge(ffn0_out, j - 1)
                    else:
                        act.wait_ge(ffn_lo, (n - 1) * NF + j - 1)
                nc.scalar.activation(hid[:, j % 2, :], F_bank[j % 2][:, 0:N], ACT.Relu,
                                     bias=vec[:, V_B1 + j:V_B1 + j + 1]).then_inc(ffn_relu, 1)

            def y_evacuate(q):
                act.wait_ge(whq_mm, q + 1)
                nc.scalar.activation(y_sb[:], L_bank[:, 0:N], ACT.Identity,
                                     bias=vec[:, V_BHQ:V_BHQ + 1]).then_inc(y2_made, 1)

            def expert_relu(q, c):
                act.wait_ge(exp_hid_mm, q * NE + c + 1)
                if c >= 2:
                    act.wait_ge(exp_lo, q * NE + c - 1)
                nc.scalar.activation(hid[:, c % 2, :], F_bank[c % 2][:, 0:N], ACT.Relu,
                                     bias=vec[:, V_E1 + c:V_E1 + c + 1]).then_inc(exp_relu, 1)

            for i in range(4):
                act.wait_ge(pre_made, i + 1)
                nc.scalar.activation(g[:].rearrange("p (t b) -> p b t", b=B)[:, 4 * i:4 * i + 4, :],
                                     pre[:, i % 2, :, :], ACT.Gelu).then_inc(g_made, 1)
            for j in range(NF):
                ffn_hidden_relu(0, j)

            def gru_chunk(k, par, experts, ffn):
                for t in range(STEPS):
                    p = t % 2
                    act.wait_ge(r_mm, k * STEPS + t + 1)
                    nc.scalar.activation(r_sb[:, p, :], R_bank[par][:, t * B:(t + 1) * B],
                                         ACT.Sigmoid).then_inc(r_made, 1)
                    act.wait_ge(z_mm, k * STEPS + t + 1)
                    nc.scalar.activation(z_sb[:, p, :], ZH_bank[par][:, t * B:(t + 1) * B],
                                         ACT.Sigmoid).then_inc(z_made, 1)
                    if experts and t == 1:
                        y_evacuate(k - 1)
                    act.wait_ge(cand_mm, k * STEPS + t + 1)
                    nc.scalar.activation(cand[:, p, :], ZH_bank[par][:, N + t * B:N + (t + 1) * B],
                                         ACT.Tanh).then_inc(cand_made, 1)
                    if ffn and t < NF:
                        ffn_hidden_relu(k + 1, t)
                    if experts and 7 <= t < 7 + NE:
                        expert_relu(k - 1, t - 7)

            gru_chunk(0, 0, False, True)
            for k in range(1, K - 1):
                gru_chunk(k, k % 2, True, True)
            gru_chunk(K - 1, (K - 1) % 2, True, False)
            y_evacuate(K - 1)
            for c in range(NE):
                expert_relu(K - 1, c)

        @block.vector
        def _(dve):
            def x1_evacuate(n):
                if isinstance(n, int) and n == 0:
                    dve.wait_ge(ffn0_out, NF)
                else:
                    dve.wait_ge(ffn_out_mm, n)
                nc.vector.scalar_tensor_tensor(
                    out=x1[:, cols(n)].rearrange("p (t b) -> p t b", b=B),
                    in0=O_bank[:, 0:N].rearrange("p (t b) -> p t b", b=B),
                    scalar=vec[:, V_B2:V_B2 + 1],
                    in1=x_sb[:, :, cols(n, STEPS)].rearrange("p b t -> p t b"),
                    op0=ALU.add, op1=ALU.add).then_inc(x1_made, 1)

            def logits(q):
                dve.wait_ge(logit_mm, q + 1)
                nc.vector.tensor_tensor(
                    lg[:], L_bank[:, N:N + 2 * E].rearrange("p (i e) -> p i e", i=2),
                    router_sb[:, 1:2, :].broadcast_to([128, 2, E]), ALU.add).then_inc(logits_made, 1)

            def best_logit(q):
                dve.wait_ge(logits_made, q + 1)
                for i in range(2):
                    nc.vector.max(top[:, i, :], lg[:, i, :]).then_inc(top_made, 1)

            def best_expert(q):
                dve.wait_ge(top_made, 2 * q + 2)
                for i in range(2):
                    nc.vector.max_index(idx[:, i, :], top[:, i, :], lg[:, i, :]).then_inc(idx_made, 1)

            def penalties(q):
                dve.wait_ge(idx_made, 2 * q + 2)
                for i in range(2):
                    nc.vector.tensor_scalar(pen[:, i, :], const_sb[:, 128:224], idx[:, i, 0:1], 1.0,
                                            ALU.is_equal, ALU.subtract).then_inc(pen_made, 1)

            def masks(q):
                dve.wait_ge(turn_mm, q + 1)
                nc.vector.tensor_copy(penT[:], maskT_ps[0:E, :]).then_inc(masks_made, 1)
                nc.vector.tensor_scalar(maskT[:], maskT_ps[0:96, :], 1.0, None, ALU.add).then_inc(masks_made, 1)

            def finish(f, par):
                dve.wait_ge(exp_out_mm, f * NE + NE)
                if not isinstance(f, int) or f >= 2:
                    dve.wait_ge(out_sent, f * 16 - 16)
                nc.vector.scalar_tensor_tensor(out=res[:, par, :], in0=O_bank[:, 0:N], scalar=0.0,
                                               in1=x1[:, cols(f)], op0=ALU.max,
                                               op1=ALU.add).then_inc(res_made, 1)

            def g_high(n):
                nc.vector.tensor_copy(g_hi[:, cols(n)], g[:, cols(n)]).then_inc(g_hi_made, 1)

            def x1_high(n):
                dve.wait_ge(x1_made, n + 1)
                nc.vector.tensor_copy(x1_hi[:], x1[:, cols(n)]).then_inc(x1_hi_made, 1)

            def ffn_high(n, j):
                dve.wait_ge(ffn_relu, n * NF + j + 1)
                nc.vector.tensor_copy(hid_hi[:, j, :], hid[:, j % 2, :]).then_inc(ffn_hi, 1)

            def y_high(q):
                dve.wait_ge(y2_made, q + 1)
                nc.vector.tensor_copy(y_hi[:], y_sb[:]).then_inc(y_hi_made, 1)

            def expert_high(q, c):
                dve.wait_ge(exp_relu, q * NE + c + 1)
                if c >= 4:
                    dve.wait_ge(exp_out_mm, q * NE + c - 3)
                nc.vector.tensor_copy(hid_hi[:, c % 4, :], hid[:, c % 2, :]).then_inc(exp_hi, 1)

            dve.wait_ge(vec_in, 16)
            nc.vector.tensor_scalar(seq_bias[:], vec[:, V_COND:V_COND + B], vec[:, V_FC:V_FC + 1], None,
                                    ALU.add).then_inc(bias_made, 1)
            h0 = vec[:, V_COND:V_COND + B]
            nc.vector.tensor_copy(hist[:, 1, (STEPS - 1) * B:N], h0).then_inc(h_made, 1)
            nc.vector.tensor_copy(m_p[:, 0, 0, :], h0).then_inc(m_hi, 1)
            dve.wait_ge(m_hi, 1)
            nc.vector.tensor_tensor(m_p[:, 0, 1, :], h0, m_p[:, 0, 0, :], ALU.subtract).then_inc(m_lo, 1)
            def effective_weights(i):
                dve.wait_ge(vv_mm, i + 1)
                nc.vector.scalar_tensor_tensor(
                    out=weff[:, 4 * i:4 * i + 4, :],
                    in0=vv_bank[i][:].rearrange("p (b c) -> p b c", b=4), scalar=LOW_RANK_SCALE,
                    in1=wt_sb[:].rearrange("p (o c) -> p o c", o=1).broadcast_to([128, 4, C]),
                    op0=ALU.mult, op1=ALU.add).then_inc(weff_made, 1)

            def pre_activations(i):
                dve.wait_ge(pre_mm, i + 1)
                if i >= 2:
                    dve.wait_ge(g_made, i - 1)
                nc.vector.tensor_tensor(
                    pre[:, i % 2, :, :], pre_bank[i][:].rearrange("p (b t) -> p b t", b=4),
                    seq_bias[:, 4 * i:4 * i + 4].rearrange("p (b o) -> p b o", o=1).broadcast_to([128, 4, T]),
                    ALU.add).then_inc(pre_made, 1)

            def below_threshold(w):
                nc.vector.tensor_scalar(below[:, w, :], ffn_sb[:, w, :], nthr[:, w:w + 1], None,
                                        ALU.is_lt).then_inc(below_made, 1)

            def ternary(w):
                dve.wait_ge(below_made, w + 1)
                nc.vector.scalar_tensor_tensor(out=wq[:, w, :], in0=ffn_sb[:, w, :], scalar=thr[:, w:w + 1],
                                               in1=below[:, w, :], op0=ALU.is_gt,
                                               op1=ALU.subtract).then_inc(wq_made, 1)

            dve.wait_ge(early_in, 16)
            effective_weights(0)
            effective_weights(1)
            dve.wait_ge(ffn_in, 16)
            nc.vector.tensor_reduce(asum[:], ffn_sb[:], AX.X, ALU.add,
                                    apply_absolute_value=True).then_inc(asum_made, 1)
            effective_weights(2)
            dve.wait_ge(gamma_mm, 1)
            nc.vector.tensor_scalar(gam[:], F_bank[0][:, 0:2], 1.0 / (FF * C), EPS,
                                    ALU.mult, ALU.add).then_inc(thr_step, 1)
            dve.wait_ge(thr_step, 1)
            nc.vector.tensor_scalar(thr[:], gam[:], 0.5, None, ALU.mult).then_inc(thr_step, 1)
            nc.vector.tensor_scalar(nthr[:], gam[:], -0.5, None, ALU.mult).then_inc(thr_step, 1)
            dve.wait_ge(thr_step, 3)
            dve.wait_ge(bias_made, 1)
            pre_activations(0)
            below_threshold(0)
            effective_weights(3)
            below_threshold(1)
            pre_activations(1)
            ternary(0)
            pre_activations(2)
            ternary(1)
            pre_activations(3)
            dve.wait_ge(wq_made, 2)
            nc.vector.tensor_copy(wq16[:], wq[:]).then_inc(wq16_made, 1)
            dve.wait_ge(gru_in, 16)
            nc.vector.tensor_copy(gru_hi[:], gru_sb[:, 0:WHQ, :]).then_inc(gru_hi_made, 1)
            dve.wait_ge(gru_hi_made, 1)
            nc.vector.tensor_tensor(gru_lo[:], gru_sb[:, 0:WHQ, :], gru_hi[:], ALU.subtract).then_inc(gru_lo_made, 1)
            dve.wait_ge(g_made, 4)
            g_high(1)
            x1_evacuate(0)

            def router_constants(t):
                if t == 1:
                    nc.vector.tensor_copy(ident[:], const_sb[:, 0:128]).then_inc(ident_made, 1)
                if t == 2:
                    dve.wait_ge(expand_in, 16)
                    nc.vector.tensor_scalar(expand_off[:], expand_sb[:], OFF, None, ALU.mult).then_inc(expand_made, 1)
                if t == 3:
                    dve.wait_ge(w1_in, 16)
                    nc.vector.tensor_copy(w1_hi[:], w1_sb[:]).then_inc(w1_hi_made, 1)
                if t == 4:
                    dve.wait_ge(w2_in, 16)
                    nc.vector.tensor_copy(w2_hi[:], w2_sb[:]).then_inc(w2_hi_made, 1)
                if t == 6:
                    nc.vector.tensor_copy(router_hi[:], router_sb[:, 0, :]).then_inc(router_hi_made, 1)
                    dve.wait_ge(b2_in, 16)
                    nc.vector.tensor_copy(b2part[:, 0, :], b2_sb[:]).then_inc(b2_step, 1)
                if t == 7:
                    dve.wait_ge(b2_step, 1)
                    nc.vector.tensor_tensor(b2res[:, 0, :], b2_sb[:], b2part[:, 0, :], ALU.subtract).then_inc(b2_step, 1)
                if t == 8:
                    dve.wait_ge(b2_step, 2)
                    nc.vector.tensor_copy(b2part[:, 1, :], b2res[:, 0, :]).then_inc(b2_step, 1)
                if t == 9:
                    dve.wait_ge(b2_step, 3)
                    nc.vector.tensor_tensor(b2res[:, 1, :], b2res[:, 0, :], b2part[:, 1, :], ALU.subtract).then_inc(b2_step, 1)
                if t == 10:
                    dve.wait_ge(b2_step, 4)
                    nc.vector.tensor_copy(b2part[:, 2, :], b2res[:, 1, :]).then_inc(b2_step, 1)
                if t == 11:
                    dve.wait_ge(b2_step, 5)
                    for i in range(3):
                        rows = slice(32 * i, 32 * i + 32)
                        nc.vector.tensor_copy(bias2_3[rows, :], b2part[rows, i, :]).then_inc(b2_step, 1)

            def gru_chunk(k, par, first, experts, ffn, fin, more_g):
                for t in range(STEPS):
                    p, q = t % 2, (t + 1) % 2
                    h_old, h_new = hist_col(par, t - 1), hist_col(par, t)
                    step = k * STEPS + t
                    dve.wait_ge(h_made, step + 1)
                    dve.wait_ge(r_made, step + 1)
                    nc.vector.tensor_tensor(rh_p[:, p, 0, :], r_sb[:, p, :], h_old, ALU.mult).then_inc(rh_hi, 1)
                    nc.vector.tensor_tensor(rh[:, p, :], r_sb[:, p, :], h_old, ALU.mult).then_inc(rh_full, 1)
                    dve.wait_ge(rh_full, step + 1)
                    nc.vector.tensor_tensor(rh_p[:, p, 1, :], rh[:, p, :], rh_p[:, p, 0, :],
                                            ALU.subtract).then_inc(rh_lo, 1)
                    dve.wait_ge(z_made, step + 1)
                    nc.vector.tensor_tensor(zh_p[:, q, 0, :], z_sb[:, p, :], h_old, ALU.mult).then_inc(zh_hi, 1)
                    nc.vector.tensor_tensor(zh[:, q, :], z_sb[:, p, :], h_old, ALU.mult).then_inc(zh_full, 1)
                    nc.vector.tensor_scalar(keep[:, p, :], z_sb[:, p, :], -1.0, 1.0,
                                            ALU.mult, ALU.add).then_inc(keep_made, 1)
                    dve.wait_ge(zh_full, step + 1)
                    nc.vector.tensor_tensor(zh_p[:, q, 1, :], zh[:, q, :], zh_p[:, q, 0, :],
                                            ALU.subtract).then_inc(zh_lo, 1)
                    dve.wait_ge(keep_made, step + 1)
                    dve.wait_ge(cand_made, step + 1)
                    nc.vector.tensor_tensor(m_p[:, q, 0, :], keep[:, p, :], cand[:, p, :], ALU.mult).then_inc(m_hi, 1)
                    nc.vector.tensor_tensor(m[:, q, :], keep[:, p, :], cand[:, p, :], ALU.mult).then_inc(m_full, 1)
                    dve.wait_ge(m_full, step + 1)
                    nc.vector.tensor_tensor(m_p[:, q, 1, :], m[:, q, :], m_p[:, q, 0, :],
                                            ALU.subtract).then_inc(m_lo, 1)
                    nc.vector.tensor_tensor(h_new, zh[:, q, :], m[:, q, :], ALU.add).then_inc(h_made, 1)
                    if first:
                        router_constants(t)
                    if fin and t == 0:
                        finish(k - 2, par)
                    if ffn and t < NF:
                        ffn_high(k + 1, t)
                    if experts:
                        if t == 1:
                            y_high(k - 1)
                        if t == 3:
                            logits(k - 1)
                            best_logit(k - 1)
                        if t == 4:
                            best_expert(k - 1)
                            penalties(k - 1)
                        if t == 6:
                            masks(k - 1)
                        if 7 <= t < 7 + NE:
                            expert_high(k - 1, t - 7)
                    if ffn and t == 5:
                        x1_evacuate(k + 1)
                        x1_high(k + 1)
                    if more_g and t == 6:
                        g_high(k + 2)

            dve.wait_ge(router_in, 16)
            gru_chunk(0, 0, True, False, True, False, True)
            gru_chunk(1, 1, False, True, True, False, True)
            for k in range(2, K - 1):
                gru_chunk(k, k % 2, False, True, True, True, k + 2 < K)
            gru_chunk(K - 1, (K - 1) % 2, False, True, False, True, False)
            y_high(K - 1)
            finish(K - 2, K % 2)
            logits(K - 1)
            best_logit(K - 1)
            best_expert(K - 1)
            penalties(K - 1)
            masks(K - 1)
            for c in range(NE):
                expert_high(K - 1, c)
            finish(K - 1, (K - 1) % 2)

        @block.tensor
        def _(pe):
            mm = nc.tensor.matmul

            def three(out, w_hi, w_lo, a_hi, a_lo, stop, wait_lo=None, shared=False):
                mm(out, w_lo, a_hi, start=False, stop=False, skip_group_check=shared)
                mm(out, w_hi, a_hi, start=False, stop=False, skip_group_check=shared)
                if wait_lo:
                    pe.wait_ge(*wait_lo)
                return mm(out, w_hi, a_lo, start=False, stop=stop, skip_group_check=shared)

            def ffn_hidden(n, j):
                if j == 0:
                    pe.wait_ge(g_hi_made, n)
                    pe.wait_ge(g_lo_made, n)
                if j >= 2:
                    pe.wait_ge(ffn_relu, n * NF + j - 1)
                w = wq16[:, 0, j * 128:(j + 1) * 128]
                mm(F_bank[j % 2][:, 0:N], w, g_hi[:, cols(n)], start=True, stop=False)
                mm(F_bank[j % 2][:, 0:N], w, g_lo[:, cols(n)], start=False, stop=True).then_inc(ffn_hid_mm, 1)

            def ffn_out(n, j):
                w = wq16[:, 1, j * 128:(j + 1) * 128]
                pe.wait_ge(ffn_hi, (n - 1) * NF + j + 1)
                mm(O_bank[:, 0:N], w, hid_hi[:, j, :], start=(j == 0), stop=False)
                pe.wait_ge(ffn_lo, (n - 1) * NF + j + 1)
                i = mm(O_bank[:, 0:N], w, hid_lo[:, j, :], start=False, stop=(j == NF - 1))
                if j == NF - 1:
                    i.then_inc(ffn_out_mm, 1)

            def project(n, par, gate):
                out = [R_bank[par][:, 0:N], ZH_bank[par][:, 0:N], ZH_bank[par][:, N:2 * N]][gate]
                mm(out, gbias3[:, gate * C:(gate + 1) * C], ones3[:], start=(gate < 2), stop=False,
                   skip_group_check=True)
                if isinstance(n, int) and n == 0:
                    mm(out, gru_sb[:, WXR + gate, :], x1[:, cols(0)], start=False, stop=False,
                       skip_group_check=True)
                    return
                if gate == 0:
                    pe.wait_ge(x1_hi_made, n)
                three(out, gru_hi[:, WXR + gate, :], gru_lo[:, WXR + gate, :], x1_hi[:], x1_lo[:], False,
                      (x1_lo_made, n) if gate == 0 else None, shared=True)

            def whq(q, par):
                mm(L_bank[:, 0:N], gru_sb[:, WHQ, :], hist[:, par, :], start=True, stop=True).then_inc(whq_mm, 1)

            def router_logits(q):
                pe.wait_ge(y_lo_made, q + 1)
                for i in range(2):
                    out, tok = L_bank[:, N + i * E:N + (i + 1) * E], slice(i * 128, (i + 1) * 128)
                    mm(out, y_lo[:, tok], router_hi[:], start=True, stop=False)
                    mm(out, y_hi[:, tok], router_hi[:], start=False, stop=False)
                    ins = mm(out, y_hi[:, tok], router_lo[:], start=False, stop=True)
                ins.then_inc(logit_mm, 1)

            def turn_masks(q):
                pe.wait_ge(pen_made, 2 * q + 2)
                for i in range(2):
                    ins = nc.tensor.transpose(maskT_ps[0:96, i * 128:(i + 1) * 128], pen[:, i, :], ident[:])
                ins.then_inc(turn_mm, 1)

            def expert_hidden(q, c):
                if c == 0:
                    pe.wait_ge(masks_made, 2 * q + 2)
                if c >= 2:
                    pe.wait_ge(exp_relu, q * NE + c - 1)
                mm(F_bank[c % 2][:, 0:N], expand_off[:, c * 128:(c + 1) * 128], penT[:], start=True, stop=False)
                block_c = slice(c * 128, (c + 1) * 128)
                three(F_bank[c % 2][:, 0:N], w1_hi[:, block_c], w1_lo[:, block_c], y_hi[:], y_lo[:],
                      True).then_inc(exp_hid_mm, 1)

            def expert_out(q, c):
                if c == 0:
                    mm(O_bank[:, 0:N], bias2_3[:], maskT[:], start=True, stop=False)
                pe.wait_ge(exp_hi, q * NE + c + 1)
                three(O_bank[:, 0:N], w2_hi[:, c, :], w2_lo[:, c, :], hid_hi[:, c % 4, :], hid_lo[:, c % 4, :],
                      c == NE - 1, (exp_lo, q * NE + c + 1)).then_inc(exp_out_mm, 1)

            def product(out, gate, part, low=False):
                if not low:
                    mm(out, gru_lo[:, WHR + gate, :], part, start=False, stop=False, skip_group_check=True)
                return mm(out, gru_hi[:, WHR + gate, :], part, start=False, stop=low, skip_group_check=True)

            def low_rank(i):
                for b in range(4 * i, 4 * i + 4):
                    ins = mm(vv_bank[i][:, (b % 4) * C:(b % 4 + 1) * C], v_sb[:, b, :], v_sb[:, b, :],
                             start=True, stop=True)
                ins.then_inc(vv_mm, 1)

            def pre_product(i):
                pe.wait_ge(weff_made, i + 1)
                pe.wait_ge(x_in[i], 16)
                for b in range(4 * i, 4 * i + 4):
                    ins = mm(pre_bank[i][:, (b % 4) * T:(b % 4 + 1) * T], weff[:, b, :], x_sb[:, b, :],
                             start=True, stop=True)
                ins.then_inc(pre_mm, 1)

            pe.wait_ge(v_in, 16)
            low_rank(0)
            low_rank(1)
            pre_product(0)
            low_rank(2)
            pe.wait_ge(asum_made, 1)
            pe.wait_ge(ones_set, 2)
            mm(F_bank[0][:, 0:2], ones[:], asum[:], start=True, stop=True).then_inc(gamma_mm, 1)
            pre_product(1)
            low_rank(3)
            pre_product(2)
            pre_product(3)
            pe.wait_ge(g_made, 4)
            pe.wait_ge(wq_made, 2)

            def first_hidden(j):
                if j >= 2:
                    pe.wait_ge(ffn_relu, j - 1)
                mm(F_bank[j % 2][:, 0:N], wq[:, 0, j * 128:(j + 1) * 128], g[:, cols(0)],
                   start=True, stop=True).then_inc(ffn_hid_mm, 1)

            def first_out(j):
                pe.wait_ge(ffn_relu, j + 1)
                mm(O_bank[:, 0:N], wq[:, 1, j * 128:(j + 1) * 128], hid[:, j % 2, :],
                   start=(j == 0), stop=(j == NF - 1)).then_inc(ffn0_out, 1)

            first_hidden(0)
            first_hidden(1)
            for j in range(NF):
                first_out(j)
                if j + 2 < NF:
                    first_hidden(j + 2)
            pe.wait_ge(gru_in, 16)
            pe.wait_ge(gb_step, 10)
            pe.wait_ge(x1_made, 1)
            for gate in range(GATES):
                project(0, 0, gate)
            pe.wait_ge(gru_lo_made, 1)
            pe.wait_ge(wq16_made, 1)

            def gru_chunk(k, par, first, experts, ffn, fin):
                for t in range(STEPS):
                    q = t % 2
                    step = k * STEPS + t
                    at = slice(t * B, (t + 1) * B)
                    r_out, z_out = R_bank[par][:, at], ZH_bank[par][:, at]
                    if not (first and t == 0):
                        pe.wait_ge(zh_lo, step)
                        product(r_out, 0, zh_p[:, q, 0, :])
                        product(r_out, 0, zh_p[:, q, 1, :], low=True)
                    pe.wait_ge(m_hi, step + 1)
                    product(r_out, 0, m_p[:, q, 0, :])
                    if not (first and t == 0):
                        product(z_out, 1, zh_p[:, q, 0, :])
                        product(z_out, 1, zh_p[:, q, 1, :], low=True)
                    product(z_out, 1, m_p[:, q, 0, :])
                    pe.wait_ge(m_lo, step + 1)
                    product(r_out, 0, m_p[:, q, 1, :], low=True).then_inc(r_mm, 1)
                    product(z_out, 1, m_p[:, q, 1, :], low=True).then_inc(z_mm, 1)
                    if ffn and t < NF:
                        ffn_hidden(k + 1, t)
                    if experts and t == 3:
                        router_logits(k - 1)
                    if experts and t == 6:
                        turn_masks(k - 1)
                    if experts and 7 <= t < 7 + NE:
                        expert_hidden(k - 1, t - 7)
                    if ffn and t == 15:
                        project(k + 1, 1 - par, 2)
                    pe.wait_ge(z_made, step + 1)
                    pe.wait_ge(rh_hi, step + 1)
                    c_out = ZH_bank[par][:, N + t * B:N + (t + 1) * B]
                    product(c_out, 2, rh_p[:, q, 0, :])
                    pe.wait_ge(rh_lo, step + 1)
                    product(c_out, 2, rh_p[:, q, 1, :], low=True).then_inc(cand_mm, 1)
                    if experts and t == 0:
                        whq(k - 1, 1 - par)
                    if fin and t == 1:
                        pe.wait_ge(res_made, k - 1)
                    if ffn and 1 <= t < 1 + NF:
                        ffn_out(k + 1, t - 1)
                    if ffn and t == 6:
                        project(k + 1, 1 - par, 0)
                    if ffn and t == 7:
                        project(k + 1, 1 - par, 1)
                    if experts and 8 <= t < 8 + NE:
                        expert_out(k - 1, t - 8)

            gru_chunk(0, 0, True, False, True, False)
            for s, n in ((ident_made, 1), (expand_made, 1), (w_lo_made, 3), (b2_step, 8)):
                pe.wait_ge(s, n)
            gru_chunk(1, 1, False, True, True, False)
            for k in range(2, K - 1):
                gru_chunk(k, k % 2, False, True, True, True)
            gru_chunk(K - 1, (K - 1) % 2, False, True, False, True)
            pe.wait_ge(h_made, K * STEPS + 1)
            whq(K - 1, (K - 1) % 2)
            router_logits(K - 1)
            turn_masks(K - 1)
            expert_hidden(K - 1, 0)
            expert_hidden(K - 1, 1)
            pe.wait_ge(res_made, K - 1)
            for c in range(NE):
                expert_out(K - 1, c)
                if c + 2 < NE:
                    expert_hidden(K - 1, c + 2)


def kernel(x, fside_Bx1x1024x16_0, cond_1024, L0_cond_W, L0_cond_fc_bias, L0_ffn_W1, L0_ffn_b1,
           L0_ffn_W2, L0_ffn_b2, L1_cond_Wxz, L1_cond_bxz, L1_cond_Whz, L1_cond_bhz, L1_cond_Wxr,
           L1_cond_bxr, L1_cond_Whr, L1_cond_bhr, L1_cond_Wxh, L1_cond_bxh, L1_cond_Whh, L1_cond_bhh,
           L1_cond_Whq, L1_cond_bhq, L1_ffn_router_w, L1_ffn_router_b, L1_ffn_weights1,
           L1_ffn_bias1, L1_ffn_weights2, L1_ffn_bias2):
    import concourse.bacc as bacc
    from concourse.bass_utils import run_bass_kernel_spmd

    a = np.asarray
    f32 = np.float32
    rows = [a(L0_cond_fc_bias)[None], a(cond_1024), a(L0_ffn_b1).reshape(NF, 128), a(L0_ffn_b2)[None],
            a(L1_cond_bhq)[None], a(L1_ffn_bias1).reshape(NE, 128)]
    arrays = {
        "xT": a(x).transpose(2, 0, 1),
        "vT": a(fside_Bx1x1024x16_0)[:, 0].transpose(2, 0, 1),
        "early": a(L0_cond_W).T,
        "vectors": np.concatenate(rows, 0).T,
        "ffn": np.stack([a(L0_ffn_W1).T, a(L0_ffn_W2).T.reshape(NF, 128, C).transpose(1, 0, 2).reshape(128, FF)], 1),
        "gru": np.stack([a(w).T for w in (L1_cond_Wxr, L1_cond_Wxz, L1_cond_Wxh, L1_cond_Whr,
                                          L1_cond_Whz, L1_cond_Whh, L1_cond_Whq)], 1),
        "gate_bias": np.stack([np.stack([np.stack([a(L1_cond_bxr), a(L1_cond_bxz), a(L1_cond_bxh)]),
                                         np.stack([a(L1_cond_bhr), a(L1_cond_bhz), a(L1_cond_bhh)])])] * 3),
        "consts": np.concatenate([np.eye(128, dtype=f32), np.tile(np.arange(E, dtype=f32), (128, 3)),
                                  np.eye(128, 3, dtype=f32)], 1),
        "expand": np.repeat(np.eye(E, dtype=f32), HE, axis=1),
        "router": np.stack([a(L1_ffn_router_w).T, np.stack([a(L1_ffn_router_b)] * 128)], 1),
        "w1": a(L1_ffn_weights1).transpose(1, 0, 2).reshape(C, E * HE),
        "w2": a(L1_ffn_weights2).reshape(NE, 128, C).transpose(1, 0, 2),
        "bias2": np.concatenate([a(L1_ffn_bias2)] * 3, 0),
    }
    arrays = {n: np.ascontiguousarray(v) for n, v in arrays.items()}

    nc = bacc.Bacc("TRN2", target_bir_lowering=False, num_devices=1)
    args = [nc.dram_tensor(n, v.shape, mybir.dt.from_np(v.dtype), kind="ExternalInput").ap()
            for n, v in arrays.items()]
    out = nc.dram_tensor("outT", (C, T * B), F32, kind="ExternalOutput").ap()
    build(nc, *args, out)
    r = run_bass_kernel_spmd(nc, [arrays], core_ids=[0])
    return np.ascontiguousarray(a(r.results[0]["outT"]).reshape(C, T, B).transpose(2, 1, 0))
```

```python
from contextlib import ExitStack

import numpy as np

import concourse.bass as bass
from concourse import mybir

F32 = mybir.dt.float32
BF16 = mybir.dt.bfloat16
F16 = mybir.dt.float16
U32 = mybir.dt.uint32
ALU = mybir.AluOpType
ACT = mybir.ActivationFunctionType
AX = mybir.AxisListType

B, T, C = 16, 128, 128
R = 16
FF = 4 * C
NF = FF // C
E, HE = 32, 32
NE = E * HE // 128
STEPS = 16
K = T // STEPS
N = STEPS * B
EPS = 1e-5
EXPERT_STEPS = dict(logits=2, best=3, choice=4, penalties=5, turn=6, hidden=7)
LAST_STEPS = dict(logits=2, best=2, choice=3, penalties=3, turn=4, hidden=5)
PRE_GROUPS = [range(0, 4), range(4, 8), range(8, 12), range(12, 14), range(14, 16)]
LOW_RANK_SCALE = 1.0 / (C * R)
KEEP_WARM = 6
OFF = 1e30

V_FC, V_COND, V_B1, V_B2, V_BHQ, V_E1 = 0, 1, 1 + B, 1 + B + NF, 2 + B + NF, 3 + B + NF
NV = V_E1 + NE
WXR, WXZ, WXH, WHR, WHZ, WHH, WHQ = range(7)
GATES = 3


def cols(k, n=N):
    return slice(k * n, (k + 1) * n) if isinstance(k, int) else bass.ds(k * n, n)


def build(nc, xT, vT, early, vectors, ffn, gru, gate_bias, consts, expand, router,
          w1, w2, bias1, bias2, outT):
    ctx = ExitStack()
    with ctx:
        def sb(name, shape, dt=F32):
            return ctx.enter_context(nc.sbuf_tensor(name, shape, dt))

        def bank(name):
            return ctx.enter_context(nc.psum_tensor(name, [128, 512], F32))

        def sem(name):
            return ctx.enter_context(nc.semaphore(name))

        x_sb = sb("x_sb", [128, B, T])
        v_sb = sb("v_sb", [R, B, C])
        wt_sb = sb("wt_sb", [128, C])
        vec = sb("vec", [128, NV])
        ffn_sb = sb("ffn_sb", [128, 2, FF])
        gru_sb = sb("gru_sb", [128, 7, C])
        gb_sb = sb("gb_sb", [3, 2, GATES, C])
        const_sb = sb("const_sb", [128, 128 + 96 + 3])
        expand_sb = sb("expand_sb", [E, NE * 128])
        router_sb = sb("router_sb", [128, 2, E])
        b1_sb = sb("b1_sb", [1, NE * 128])
        w1_sb = sb("w1_sb", [128, NE * 128])
        w2_sb = sb("w2_sb", [128, NE, C])
        b2_sb = sb("b2_sb", [96, C])

        weff = sb("weff", [128, B, C])
        seq_bias = sb("seq_bias", [128, B])
        pre = sb("pre", [128, 3, 4, T])
        g = sb("g", [128, T * B])
        g_hi = sb("g_hi", [128, T * B], F16)
        g_lo = sb("g_lo", [128, T * B], F16)
        ones = sb("ones", [128, 128])
        ones3 = sb("ones3", [3, N], BF16)
        asum = sb("asum", [128, 2])
        gam = sb("gam", [128, 2])
        thr = sb("thr", [128, 2])
        nthr = sb("nthr", [128, 2])
        below = sb("below", [128, 2, FF], F16)
        wq16 = sb("wq16", [128, 2, FF], F16)
        wq = sb("wq", [128, 2, FF])
        gsum = sb("gsum", [3, GATES * C])
        gres = sb("gres", [3, 2, GATES * C])
        gpart = sb("gpart", [3, 2, GATES * C], BF16)
        gpick = sb("gpick", [3, 4, GATES * C], BF16)
        gbias3 = sb("gbias3", [3, GATES * C], BF16)
        gru_hi = sb("gru_hi", [128, WHQ, C], F16)
        gru_lo = sb("gru_lo", [128, WHQ, C], F16)
        w1_hi = sb("w1_hi", [128, NE * 128], F16)
        w1_lo = sb("w1_lo", [128, NE * 128], F16)
        w2_hi = sb("w2_hi", [128, NE, C], F16)
        w2_lo = sb("w2_lo", [128, NE, C], F16)
        router_hi = sb("router_hi", [128, E], F16)
        router_lo = sb("router_lo", [128, E], F16)
        ident = sb("ident", [128, 128], BF16)
        expand_off = sb("expand_off", [E + 3, NE * 128], BF16)
        b1res = sb("b1res", [1, 2, NE * 128])
        b1part = sb("b1part", [1, 3, NE * 128], BF16)
        b2res = sb("b2res", [96, 2, C])
        b2part = sb("b2part", [96, 3, C], BF16)
        b2pick = sb("b2pick", [96, 2, C], BF16)
        bias2_3 = sb("bias2_3", [96, C], BF16)

        x1 = sb("x1", [128, T * B])
        x1_hi = sb("x1_hi", [128, N], F16)
        x1_lo = sb("x1_lo", [128, N], F16)
        hid = sb("hid", [128, 2, N])
        hid_hi = sb("hid_hi", [128, 4, N], F16)
        hid_lo = sb("hid_lo", [128, 4, N], F16)
        hist = sb("hist", [128, 2, N])
        y_sb = sb("y_sb", [128, N])
        y_hi = sb("y_hi", [128, N], F16)
        y_lo = sb("y_lo", [128, N], F16)
        lg = sb("lg", [128, 2, E])
        top = sb("top", [128, 2, 8])
        idx = sb("idx", [128, 2, 8], U32)
        pen = sb("pen", [128, 2, 96], BF16)
        penT = sb("penT", [E, N], BF16)
        maskT = sb("maskT", [96, N], BF16)
        res = sb("res", [128, 2, N])

        y_last = sb("y_last", [128, 2, 128])
        y_last_hi = sb("y_last_hi", [128, 2, 128], F16)
        y_last_lo = sb("y_last_lo", [128, 2, 128], F16)
        lg_last = sb("lg_last", [128, 2, E])
        top_last = sb("top_last", [128, 2, 8])
        idx_last = sb("idx_last", [128, 2, 8], U32)
        pen_last = sb("pen_last", [128, 2, 96], BF16)
        penT_last = sb("penT_last", [E + 3, 2, 128], BF16)
        maskT_last = sb("maskT_last", [96, 2, 128], BF16)
        hid_last_hi = sb("hid_last_hi", [128, 2, NE, 128], F16)
        hid_last_lo = sb("hid_last_lo", [128, 2, NE, 128], F16)

        r_sb = sb("r_sb", [128, 2, B])
        z_sb = sb("z_sb", [128, 2, B])
        cand = sb("cand", [128, 2, B])
        keep = sb("keep", [128, 2, B])
        rh = sb("rh", [128, 2, B])
        zh = sb("zh", [128, 2, B])
        m = sb("m", [128, 2, B])
        rh_p = sb("rh_p", [128, 2, 2, B], F16)
        zh_p = sb("zh_p", [128, 2, 2, B], F16)
        m_p = sb("m_p", [128, 2, 2, B], F16)

        R_bank = [bank("R0"), bank("R1")]
        ZH_bank = [bank("ZH0"), bank("ZH1")]
        F_bank = [bank("F0"), bank("F1")]
        O_bank = bank("O")
        L_bank = bank("L")
        vv_bank = [F_bank[0], F_bank[1], R_bank[0], R_bank[1]]
        pre_bank = [ZH_bank[0], ZH_bank[1], O_bank, L_bank, R_bank[0]]
        maskT_ps = L_bank[:, 320:320 + N // 2].bitcast(BF16)

        last_hid_bank = [R_bank[0], ZH_bank[0], F_bank[0], F_bank[1]]
        last_out_bank = [R_bank[1], ZH_bank[1]]

        x_in = [sem(f"x_in{i}") for i in range(4)]
        v_first_in = sem("v_first_in")
        v_in, early_in, vec_in, ffn_in, gru_in = (sem(n) for n in
            ("v_in", "early_in", "vec_in", "ffn_in", "gru_in"))
        gb_in, const_in, expand_in, router_in, w1_in, w2_in, b2_in = (sem(n) for n in
            ("gb_in", "const_in", "expand_in", "router_in", "w1_in", "w2_in", "b2_in"))
        ones_set = sem("ones_set")
        vv_mm, weff_made, pre_mm, pre_made, g_made = (sem(n) for n in
            ("vv_mm", "weff_made", "pre_mm", "pre_made", "g_made"))
        bias_made, asum_made, gamma_mm, thr_step, below_made, wq_made = (sem(n) for n in
            ("bias_made", "asum_made", "gamma_mm", "thr_step", "below_made", "wq_made"))
        gb_step, b2_step, ident_made, expand_made = (sem(n) for n in
            ("gb_step", "b2_step", "ident_made", "expand_made"))
        ffn_hid_mm, ffn_relu, ffn_out_mm, x1_made = (sem(n) for n in
            ("ffn_hid_mm", "ffn_relu", "ffn_out_mm", "x1_made"))
        proj_mm = sem("proj_mm")
        whq_mm, y2_made, logit_mm, logits_made, top_made, idx_made, pen_made = (sem(n) for n in
            ("whq_mm", "y2_made", "logit_mm", "logits_made", "top_made", "idx_made", "pen_made"))
        turn_mm, masks_made, exp_hid_mm, exp_relu, exp_out_mm, res_made, out_sent = (sem(n) for n in
            ("turn_mm", "masks_made", "exp_hid_mm", "exp_relu", "exp_out_mm", "res_made", "out_sent"))
        r_mm, z_mm, cand_mm = sem("r_mm"), sem("z_mm"), sem("cand_mm")
        r_made, z_made, cand_made = sem("r_made"), sem("z_made"), sem("cand_made")
        keep_made, h_made = sem("keep_made"), sem("h_made")
        rh_full, zh_full, m_full = sem("rh_full"), sem("zh_full"), sem("m_full")
        rh_hi, zh_hi, m_hi = sem("rh_hi"), sem("zh_hi"), sem("m_hi")
        rh_lo, zh_lo, m_lo = sem("rh_lo"), sem("zh_lo"), sem("m_lo")
        gru_hi_made, gru_lo_made = sem("gru_hi_made"), sem("gru_lo_made")
        wq16_made, ffn0_out = sem("wq16_made"), sem("ffn0_out")
        w1_hi_made, w2_hi_made, router_hi_made, w_lo_made = (sem(n) for n in
            ("w1_hi_made", "w2_hi_made", "router_hi_made", "w_lo_made"))
        g_hi_made, g_lo_made, x1_hi_made, x1_lo_made = (sem(n) for n in
            ("g_hi_made", "g_lo_made", "x1_hi_made", "x1_lo_made"))
        ffn_hi, ffn_lo, exp_hi, exp_lo, y_hi_made, y_lo_made = (sem(n) for n in
            ("ffn_hi", "ffn_lo", "exp_hi", "exp_lo", "y_hi_made", "y_lo_made"))

        b1_in, b1_step, b1_rows, b1_ones = (sem(n) for n in ("b1_in", "b1_step", "b1_rows", "b1_ones"))
        last_y_mm, last_y, last_y_hi, last_y_lo, last_logit_mm, last_logits, last_top, last_idx = (
            sem("last_" + n) for n in ("y_mm", "y", "y_hi", "y_lo", "logit_mm", "logits", "top", "idx"))
        last_pen, last_turn_mm, last_masks, last_hid_mm, last_hi, last_lo, last_out_mm, last_res, last_sent = (
            sem("last_" + n) for n in ("pen", "turn_mm", "masks", "hid_mm", "hi", "lo", "out_mm", "res", "sent"))

        block = ctx.enter_context(nc.Block())

        def hist_col(par, t):
            if t < 0:
                par, t = 1 - par, STEPS - 1
            return hist[:, par, t * B:(t + 1) * B]

        @block.sync
        def _(sp):
            sp.dma_start(v_sb[:, 0:4, :], vT[:, 0:4, :]).then_inc(v_first_in, 16)
            sp.dma_start(v_sb[:, 4:B, :], vT[:, 4:B, :]).then_inc(v_in, 16)
            for i in range(4):
                sp.dma_start(x_sb[:, 4 * i:4 * i + 4, :], xT[:, 4 * i:4 * i + 4, :]).then_inc(x_in[i], 16)
            sp.dma_start(router_sb[:], router).then_inc(router_in, 16)
            sp.dma_start(w2_sb[:], w2).then_inc(w2_in, 16)
            sp.dma_start(b2_sb[:], bias2).then_inc(b2_in, 16)
            sp.dma_start(b1_sb[:], bias1).then_inc(b1_in, 16)

            def store(f, par):
                sp.wait_ge(res_made, f + 1)
                sp.dma_start(outT[:, cols(f)], res[:, par, :]).then_inc(out_sent, 16)
                sp.wait_ge(out_sent, 16 * f + 48)

            for f in range(K - 1):
                store(f, f % 2)
                if f == 4:
                    sp.wait_ge(b1_step, 5 * NE * 128 // N)
                    for i in range(3):
                        sp.dma_start(expand_off[E + i:E + i + 1, :], b1part[:, i, :]).then_inc(b1_rows, 16)
            for h in range(2):
                sp.wait_ge(last_res, h + 1)
                sp.dma_start(outT[:, (K - 1) * N + h * 128:(K - 1) * N + (h + 1) * 128],
                             res[:, (K - 1) % 2, h * 128:(h + 1) * 128]).then_inc(last_sent, 16)
            sp.wait_ge(last_sent, 32)

        @block.gpsimd
        def _(pool):
            pool.dma_start(gb_sb[:], gate_bias).then_inc(gb_in, 16)
            pool.dma_start(const_sb[:], consts).then_inc(const_in, 16)
            nc.gpsimd.memset(ones[:], 1.0).then_inc(ones_set, 1)
            nc.gpsimd.memset(ones3[:], 1.0).then_inc(ones_set, 1)

            def g_low(n):
                pool.wait_ge(g_hi_made, n)
                nc.gpsimd.tensor_tensor(g_lo[:, cols(n)], g[:, cols(n)], g_hi[:, cols(n)],
                                        ALU.subtract).then_inc(g_lo_made, 1)

            def x1_low(n):
                pool.wait_ge(x1_hi_made, n)
                nc.gpsimd.tensor_tensor(x1_lo[:], x1[:, cols(n)], x1_hi[:], ALU.subtract).then_inc(x1_lo_made, 1)

            def ffn_low(n, j):
                pool.wait_ge(ffn_hi, (n - 1) * NF + j + 1)
                nc.gpsimd.tensor_tensor(hid_lo[:, j, :], hid[:, j % 2, :], hid_hi[:, j, :],
                                        ALU.subtract).then_inc(ffn_lo, 1)

            def expert_low(q, c):
                pool.wait_ge(exp_hi, q * NE + c + 1)
                nc.gpsimd.tensor_tensor(hid_lo[:, c % 4, :], hid[:, c % 2, :], hid_hi[:, c % 4, :],
                                        ALU.subtract).then_inc(exp_lo, 1)

            pool.wait_ge(gb_in, 16)
            pool.wait_ge(const_in, 16)
            flat = gb_sb[:].rearrange("p s g c -> p s (g c)")
            pick = const_sb[:, 224:227]
            t_t, t_s = nc.gpsimd.tensor_tensor, nc.gpsimd.tensor_scalar
            t_t(gsum[:], flat[:, 0, :], flat[:, 1, :], ALU.add).then_inc(gb_step, 1)
            pool.wait_ge(gb_step, 1)
            t_s(gpart[:, 0, :], gsum[:], 0.0, None, ALU.add).then_inc(gb_step, 1)
            pool.wait_ge(gb_step, 2)
            t_t(gres[:, 0, :], gsum[:], gpart[:, 0, :], ALU.subtract).then_inc(gb_step, 1)
            pool.wait_ge(gb_step, 3)
            t_s(gpart[:, 1, :], gres[:, 0, :], 0.0, None, ALU.add).then_inc(gb_step, 1)
            pool.wait_ge(gb_step, 4)
            t_t(gres[:, 1, :], gres[:, 0, :], gpart[:, 1, :], ALU.subtract).then_inc(gb_step, 1)
            t_s(gpick[:, 0, :], gpart[:, 0, :], pick[0:3, 0:1], None, ALU.mult).then_inc(gb_step, 1)
            t_s(gpick[:, 1, :], gpart[:, 1, :], pick[0:3, 1:2], None, ALU.mult).then_inc(gb_step, 1)
            pool.wait_ge(gb_step, 7)
            t_s(gpick[:, 2, :], gres[:, 1, :], pick[0:3, 2:3], None, ALU.mult).then_inc(gb_step, 1)
            t_t(gpick[:, 3, :], gpick[:, 0, :], gpick[:, 1, :], ALU.add).then_inc(gb_step, 1)
            pool.wait_ge(gb_step, 9)
            t_t(gbias3[:], gpick[:, 2, :], gpick[:, 3, :], ALU.add).then_inc(gb_step, 1)
            g_low(1)

            def chunk(k, first, experts, ffn, more_g):
                if ffn:
                    for j in range(NF):
                        ffn_low(k + 1, j)
                    x1_low(k + 1)
                if more_g and first:
                    g_low(k + 2)
                if first:
                    for hi_made, full, hi, lo in ((w1_hi_made, w1_sb[:], w1_hi[:], w1_lo[:]),
                                                  (w2_hi_made, w2_sb[:], w2_hi[:], w2_lo[:]),
                                                  (router_hi_made, router_sb[:, 0, :], router_hi[:], router_lo[:])):
                        pool.wait_ge(hi_made, 1 if hi_made is router_hi_made else 2)
                        nc.gpsimd.tensor_tensor(lo, full, hi, ALU.subtract).then_inc(w_lo_made, 1)
                if experts:
                    for c in range(NE):
                        expert_low(k - 1, c)
                        if more_g and c == 2:
                            g_low(k + 2)

            chunk(0, True, False, True, True)
            chunk(1, False, True, True, True)
            with pool.Fori(1, K // 2 - 1) as j:
                chunk(2 * j, False, True, True, True)
                chunk(2 * j + 1, False, True, True, True)
            chunk(K - 2, False, True, True, False)
            chunk(K - 1, False, True, False, False)

        @block.scalar
        def _(act):
            act.dma_start(wt_sb[:], early).then_inc(early_in, 16)
            act.dma_start(vec[:], vectors).then_inc(vec_in, 16)
            act.dma_start(ffn_sb[:], ffn).then_inc(ffn_in, 16)
            act.dma_start(gru_sb[:], gru).then_inc(gru_in, 16)
            act.dma_start(expand_sb[:], expand).then_inc(expand_in, 16)
            act.dma_start(w1_sb[:], w1).then_inc(w1_in, 16)

            def ffn_hidden_relu(n, j):
                act.wait_ge(ffn_hid_mm, n * NF + j + 1)
                if j >= 2:
                    if isinstance(n, int) and n == 0:
                        act.wait_ge(ffn0_out, j - 1)
                    else:
                        act.wait_ge(ffn_lo, (n - 1) * NF + j - 1)
                nc.scalar.activation(hid[:, j % 2, :], F_bank[j % 2][:, 0:N], ACT.Relu,
                                     bias=vec[:, V_B1 + j:V_B1 + j + 1]).then_inc(ffn_relu, 1)

            def ffn_hidden_high(n, j):
                nc.scalar.activation(hid_hi[:, j, :], F_bank[j % 2][:, 0:N], ACT.Relu,
                                     bias=vec[:, V_B1 + j:V_B1 + j + 1]).then_inc(ffn_hi, 1)

            def y_evacuate(q):
                act.wait_ge(whq_mm, q + 1)
                nc.scalar.activation(y_sb[:], L_bank[:, 0:N], ACT.Identity,
                                     bias=vec[:, V_BHQ:V_BHQ + 1]).then_inc(y2_made, 1)

            def expert_relu(q, c):
                act.wait_ge(exp_hid_mm, q * NE + c + 1)
                if c >= 2:
                    act.wait_ge(exp_lo, q * NE + c - 1)
                nc.scalar.activation(hid[:, c % 2, :], F_bank[c % 2][:, 0:N], ACT.Relu,
                                     bias=vec[:, V_E1 + c:V_E1 + c + 1]).then_inc(exp_relu, 1)

            def last_y_evacuate(h):
                act.wait_ge(last_y_mm, h + 1)
                nc.scalar.activation(y_last[:, h, :], L_bank[:, 0:128], ACT.Identity,
                                     bias=vec[:, V_BHQ:V_BHQ + 1]).then_inc(last_y, 1)

            def last_relu(h, c):
                act.wait_ge(last_hid_mm, h * NE + c + 2)
                nc.scalar.activation(hid_last_hi[:, h, c:c + 2, :],
                                     last_hid_bank[c // 2][:, 0:256].rearrange("p (c n) -> p c n", c=2),
                                     ACT.Relu).then_inc(last_hi, 1)

            for i, seqs in enumerate(PRE_GROUPS):
                act.wait_ge(pre_made, i + 1)
                nc.scalar.activation(g[:].rearrange("p (t b) -> p b t", b=B)[:, seqs.start:seqs.stop, :],
                                     pre[:, i % 3, 0:len(seqs), :], ACT.Gelu).then_inc(g_made, 1)
            for j in range(NF):
                ffn_hidden_relu(0, j)

            def gru_chunk(k, par, experts, ffn, last=False):
                at = LAST_STEPS if last else EXPERT_STEPS
                for t in range(STEPS):
                    p = t % 2
                    act.wait_ge(r_mm, k * STEPS + t + 1)
                    nc.scalar.activation(r_sb[:, p, :], R_bank[par][:, t * B:(t + 1) * B],
                                         ACT.Sigmoid).then_inc(r_made, 1)
                    act.wait_ge(z_mm, k * STEPS + t + 1)
                    nc.scalar.activation(z_sb[:, p, :], ZH_bank[par][:, t * B:(t + 1) * B],
                                         ACT.Sigmoid).then_inc(z_made, 1)
                    if experts and t == 1:
                        y_evacuate(k - 1)
                    if last and t == 9:
                        last_y_evacuate(0)
                    act.wait_ge(cand_mm, k * STEPS + t + 1)
                    nc.scalar.activation(cand[:, p, :], ZH_bank[par][:, N + t * B:N + (t + 1) * B],
                                         ACT.Tanh).then_inc(cand_made, 1)
                    if ffn and t < NF:
                        ffn_hidden_relu(k + 1, t)
                        ffn_hidden_high(k + 1, t)
                    if experts and at["hidden"] <= t < at["hidden"] + NE:
                        expert_relu(k - 1, t - at["hidden"])
                    if last and 13 <= t:
                        last_relu(0, 2 * (t - 13))

            gru_chunk(0, 0, False, True)
            gru_chunk(1, 1, True, True)
            with act.Fori(1, K // 2 - 1) as j:
                gru_chunk(2 * j, 0, True, True)
                gru_chunk(2 * j + 1, 1, True, True)
            gru_chunk(K - 2, 0, True, True)
            gru_chunk(K - 1, (K - 1) % 2, True, False, last=True)
            last_y_evacuate(1)
            last_relu(0, 6)
            for c in range(0, NE, 2):
                last_relu(1, c)

        @block.vector
        def _(dve):
            def x1_evacuate(n):
                if isinstance(n, int) and n == 0:
                    dve.wait_ge(ffn0_out, NF)
                else:
                    dve.wait_ge(ffn_out_mm, n)
                nc.vector.scalar_tensor_tensor(
                    out=x1[:, cols(n)].rearrange("p (t b) -> p t b", b=B),
                    in0=O_bank[:, 0:N].rearrange("p (t b) -> p t b", b=B),
                    scalar=vec[:, V_B2:V_B2 + 1],
                    in1=x_sb[:, :, cols(n, STEPS)].rearrange("p b t -> p t b"),
                    op0=ALU.add, op1=ALU.add).then_inc(x1_made, 1)

            def logits(q):
                dve.wait_ge(logit_mm, q + 1)
                nc.vector.tensor_tensor(
                    lg[:], L_bank[:, N:N + 2 * E].rearrange("p (i e) -> p i e", i=2),
                    router_sb[:, 1:2, :].broadcast_to([128, 2, E]), ALU.add).then_inc(logits_made, 1)

            def best_logit(q):
                for i in range(2):
                    nc.vector.max(top[:, i, :], lg[:, i, :]).then_inc(top_made, 1)

            def best_expert(q):
                for i in range(2):
                    nc.vector.max_index(idx[:, i, :], top[:, i, :], lg[:, i, :]).then_inc(idx_made, 1)

            def penalties(q):
                dve.wait_ge(idx_made, 2 * q + 2)
                for i in range(2):
                    nc.vector.tensor_scalar(pen[:, i, :], const_sb[:, 128:224], idx[:, i, 0:1], 1.0,
                                            ALU.is_equal, ALU.subtract).then_inc(pen_made, 1)

            def masks(q):
                dve.wait_ge(turn_mm, q + 1)
                nc.vector.tensor_copy(penT[:], maskT_ps[0:E, :]).then_inc(masks_made, 1)
                nc.vector.tensor_scalar(maskT[:], maskT_ps[0:96, :], 1.0, None, ALU.add).then_inc(masks_made, 1)

            def finish(f, par):
                dve.wait_ge(exp_out_mm, f * NE + NE)
                dve.wait_ge(out_sent, 16 * f + 16)
                nc.vector.scalar_tensor_tensor(out=res[:, par, :], in0=O_bank[:, 0:N], scalar=0.0,
                                               in1=x1[:, cols(f)], op0=ALU.max,
                                               op1=ALU.add).then_inc(res_made, 1)

            def g_high(n):
                nc.vector.tensor_scalar(g_hi[:, cols(n)], g[:, cols(n)], 1.0, None, ALU.mult).then_inc(g_hi_made, 1)

            def x1_high(n):
                dve.wait_ge(x1_made, n + 1)
                nc.vector.tensor_scalar(x1_hi[:], x1[:, cols(n)], 1.0, None, ALU.mult).then_inc(x1_hi_made, 1)

            def y_high(q):
                dve.wait_ge(y2_made, q + 1)
                nc.vector.tensor_copy(y_hi[:], y_sb[:]).then_inc(y_hi_made, 1)

            def y_low(q):
                dve.wait_ge(y_hi_made, q + 1)
                nc.vector.tensor_tensor(y_lo[:], y_sb[:], y_hi[:], ALU.subtract).then_inc(y_lo_made, 1)

            def expert_high(q, c):
                dve.wait_ge(exp_relu, q * NE + c + 1)
                if c >= 4:
                    dve.wait_ge(exp_out_mm, q * NE + c - 3)
                nc.vector.tensor_copy(hid_hi[:, c % 4, :], hid[:, c % 2, :]).then_inc(exp_hi, 1)

            def last_y_high(h):
                dve.wait_ge(last_y, h + 1)
                nc.vector.tensor_copy(y_last_hi[:, h, :], y_last[:, h, :]).then_inc(last_y_hi, 1)

            def last_y_low(h):
                dve.wait_ge(last_y_hi, h + 1)
                nc.vector.tensor_tensor(y_last_lo[:, h, :], y_last[:, h, :], y_last_hi[:, h, :],
                                        ALU.subtract).then_inc(last_y_lo, 1)

            def last_best_logit(h):
                dve.wait_ge(last_logit_mm, h + 1)
                nc.vector.tensor_tensor(lg_last[:, h, :], L_bank[:, N:N + E], router_sb[:, 1, :],
                                        ALU.add).then_inc(last_logits, 1)
                dve.wait_ge(last_logits, h + 1)
                nc.vector.max(top_last[:, h, :], lg_last[:, h, :]).then_inc(last_top, 1)

            def last_best_expert(h):
                dve.wait_ge(last_top, h + 1)
                nc.vector.max_index(idx_last[:, h, :], top_last[:, h, :], lg_last[:, h, :]).then_inc(last_idx, 1)

            def last_penalties(h):
                dve.wait_ge(last_idx, h + 1)
                nc.vector.tensor_scalar(pen_last[:, h, :], const_sb[:, 128:224], idx_last[:, h, 0:1], 1.0,
                                        ALU.is_equal, ALU.subtract).then_inc(last_pen, 1)

            def make_last_masks(h):
                dve.wait_ge(last_turn_mm, h + 1)
                nc.vector.tensor_copy(penT_last[0:E, h, :], maskT_ps[0:E, 0:128]).then_inc(last_masks, 1)
                nc.vector.tensor_scalar(maskT_last[:, h, :], maskT_ps[0:96, 0:128], 1.0, None,
                                        ALU.add).then_inc(last_masks, 1)

            def last_low(h, c):
                dve.wait_ge(last_hi, (h * NE + c) // 2 + 1)
                nc.vector.scalar_tensor_tensor(
                    out=hid_last_lo[:, h, c:c + 2, :],
                    in0=last_hid_bank[c // 2][:, 0:256].rearrange("p (c n) -> p c n", c=2), scalar=0.0,
                    in1=hid_last_hi[:, h, c:c + 2, :], op0=ALU.max, op1=ALU.subtract).then_inc(last_lo, 1)

            def last_finish(h):
                dve.wait_ge(last_out_mm, h + 1)
                if h == 0:
                    dve.wait_ge(out_sent, K * 16)
                half = slice(h * 128, (h + 1) * 128)
                nc.vector.scalar_tensor_tensor(
                    out=res[:, (K - 1) % 2, half], in0=last_out_bank[h][:, 0:128], scalar=0.0,
                    in1=x1[:, (K - 1) * N + h * 128:(K - 1) * N + (h + 1) * 128],
                    op0=ALU.max, op1=ALU.add).then_inc(last_res, 1)

            nc.vector.memset(res[:], 0.0).then_inc(out_sent, 32)
            dve.wait_ge(vec_in, 16)
            nc.vector.tensor_scalar(seq_bias[:], vec[:, V_COND:V_COND + B], vec[:, V_FC:V_FC + 1], None,
                                    ALU.add).then_inc(bias_made, 1)
            h0 = vec[:, V_COND:V_COND + B]
            nc.vector.tensor_copy(hist[:, 1, (STEPS - 1) * B:N], h0).then_inc(h_made, 1)
            nc.vector.tensor_copy(m_p[:, 0, 0, :], h0).then_inc(m_hi, 1)
            dve.wait_ge(m_hi, 1)
            nc.vector.tensor_tensor(m_p[:, 0, 1, :], h0, m_p[:, 0, 0, :], ALU.subtract).then_inc(m_lo, 1)
            def effective_weights(i):
                dve.wait_ge(vv_mm, i + 1)
                nc.vector.scalar_tensor_tensor(
                    out=weff[:, 4 * i:4 * i + 4, :],
                    in0=vv_bank[i][:].rearrange("p (b c) -> p b c", b=4), scalar=LOW_RANK_SCALE,
                    in1=wt_sb[:].rearrange("p (o c) -> p o c", o=1).broadcast_to([128, 4, C]),
                    op0=ALU.mult, op1=ALU.add).then_inc(weff_made, 1)

            def pre_activations(i):
                dve.wait_ge(pre_mm, i + 1)
                if i >= 3:
                    dve.wait_ge(g_made, i - 2)
                seqs, n = PRE_GROUPS[i], len(PRE_GROUPS[i])
                nc.vector.tensor_tensor(
                    pre[:, i % 3, 0:n, :], pre_bank[i][:, 0:n * T].rearrange("p (b t) -> p b t", b=n),
                    seq_bias[:, seqs.start:seqs.stop].rearrange("p (b o) -> p b o", o=1).broadcast_to([128, n, T]),
                    ALU.add).then_inc(pre_made, 1)

            def below_threshold(w):
                nc.vector.tensor_scalar(below[:, w, :], ffn_sb[:, w, :], nthr[:, w:w + 1], None,
                                        ALU.is_lt).then_inc(below_made, 1)

            def ternary(w):
                dve.wait_ge(below_made, w + 1)
                nc.vector.scalar_tensor_tensor(out=wq[:, w, :], in0=ffn_sb[:, w, :], scalar=thr[:, w:w + 1],
                                               in1=below[:, w, :], op0=ALU.is_gt,
                                               op1=ALU.subtract).then_inc(wq_made, 1)

            dve.wait_ge(early_in, 16)
            effective_weights(0)
            effective_weights(1)
            dve.wait_ge(ffn_in, 16)
            nc.vector.tensor_reduce(asum[:], ffn_sb[:], AX.X, ALU.add,
                                    apply_absolute_value=True).then_inc(asum_made, 1)
            effective_weights(2)
            effective_weights(3)
            dve.wait_ge(gamma_mm, 1)
            nc.vector.tensor_scalar(gam[:], F_bank[0][:, 0:2], 1.0 / (FF * C), EPS,
                                    ALU.mult, ALU.add).then_inc(thr_step, 1)
            dve.wait_ge(thr_step, 1)
            nc.vector.tensor_scalar(thr[:], gam[:], 0.5, None, ALU.mult).then_inc(thr_step, 1)
            nc.vector.tensor_scalar(nthr[:], gam[:], -0.5, None, ALU.mult).then_inc(thr_step, 1)
            dve.wait_ge(thr_step, 3)
            dve.wait_ge(bias_made, 1)
            below_threshold(0)
            below_threshold(1)
            pre_activations(0)
            ternary(0)
            for i in range(1, len(PRE_GROUPS)):
                pre_activations(i)
            ternary(1)
            dve.wait_ge(wq_made, 2)
            nc.vector.tensor_copy(wq16[:], wq[:]).then_inc(wq16_made, 1)
            dve.wait_ge(gru_in, 16)
            nc.vector.tensor_copy(gru_hi[:], gru_sb[:, 0:WHQ, :]).then_inc(gru_hi_made, 1)
            dve.wait_ge(gru_hi_made, 1)
            nc.vector.tensor_tensor(gru_lo[:], gru_sb[:, 0:WHQ, :], gru_hi[:], ALU.subtract).then_inc(gru_lo_made, 1)
            dve.wait_ge(g_made, len(PRE_GROUPS))
            g_high(1)
            x1_evacuate(0)

            def router_constants(t):
                if t == 1:
                    nc.vector.tensor_copy(ident[:], const_sb[:, 0:128]).then_inc(ident_made, 1)
                if t in (2, 3):
                    dve.wait_ge(expand_in, 16)
                    half = slice((t - 2) * 512, (t - 1) * 512)
                    nc.vector.tensor_scalar(expand_off[0:E, half], expand_sb[:, half], OFF, None,
                                            ALU.mult).then_inc(expand_made, 1)
                if t in (5, 7):
                    dve.wait_ge(w1_in, 16)
                    half = slice((t // 6) * 512, (t // 6 + 1) * 512)
                    nc.vector.tensor_copy(w1_hi[:, half], w1_sb[:, half]).then_inc(w1_hi_made, 1)
                if t in (8, 9):
                    dve.wait_ge(w2_in, 16)
                    half = slice((t - 8) * NE // 2, (t - 7) * NE // 2)
                    nc.vector.tensor_copy(w2_hi[:, half, :], w2_sb[:, half, :]).then_inc(w2_hi_made, 1)
                if t == 12:
                    nc.vector.memset(penT_last[E:E + 3, :, :], 1.0).then_inc(b1_ones, 1)
                if t == 6:
                    nc.vector.tensor_copy(router_hi[:], router_sb[:, 0, :]).then_inc(router_hi_made, 1)
                    dve.wait_ge(b2_in, 16)
                    nc.vector.tensor_copy(b2part[:, 0, :], b2_sb[:]).then_inc(b2_step, 1)
                if t == 7:
                    dve.wait_ge(b2_step, 1)
                    nc.vector.tensor_tensor(b2res[:, 0, :], b2_sb[:], b2part[:, 0, :], ALU.subtract).then_inc(b2_step, 1)
                if t == 10:
                    dve.wait_ge(b2_step, 2)
                    nc.vector.tensor_copy(b2part[:, 1, :], b2res[:, 0, :]).then_inc(b2_step, 1)
                if t == 11:
                    dve.wait_ge(b2_step, 3)
                    nc.vector.tensor_tensor(b2res[:, 1, :], b2res[:, 0, :], b2part[:, 1, :], ALU.subtract).then_inc(b2_step, 1)
                if t == 13:
                    dve.wait_ge(b2_step, 4)
                    nc.vector.tensor_copy(b2part[:, 2, :], b2res[:, 1, :]).then_inc(b2_step, 1)
                if t == 14:
                    dve.wait_ge(b2_step, 5)
                    for i in range(3):
                        rows = slice(32 * i, 32 * i + 32)
                        nc.vector.tensor_copy(bias2_3[rows, :], b2part[rows, i, :]).then_inc(b2_step, 1)

            def bias1_parts(quarter, i):
                at = cols(quarter)
                if i == 0:
                    dve.wait_ge(b1_in, 16)
                else:
                    dve.wait_ge(b1_step, 5 * quarter + i)
                parts, rest = b1part[:, :, at], b1res[:, :, at]
                if i == 0:
                    ins = nc.vector.tensor_copy(parts[:, 0, :], b1_sb[:, at])
                if i == 1:
                    ins = nc.vector.tensor_tensor(rest[:, 0, :], b1_sb[:, at], parts[:, 0, :], ALU.subtract)
                if i == 2:
                    ins = nc.vector.tensor_copy(parts[:, 1, :], rest[:, 0, :])
                if i == 3:
                    ins = nc.vector.tensor_tensor(rest[:, 1, :], rest[:, 0, :], parts[:, 1, :], ALU.subtract)
                if i == 4:
                    ins = nc.vector.tensor_copy(parts[:, 2, :], rest[:, 1, :])
                ins.then_inc(b1_step, 1)

            def gru_chunk(k, par, first, experts, ffn, fin, more_g, last=False):
                at = LAST_STEPS if last else EXPERT_STEPS
                for t in range(STEPS):
                    p, q = t % 2, (t + 1) % 2
                    h_old, h_new = hist_col(par, t - 1), hist_col(par, t)
                    step = k * STEPS + t
                    dve.wait_ge(h_made, step + 1)
                    dve.wait_ge(r_made, step + 1)
                    nc.vector.tensor_tensor(rh_p[:, p, 0, :], r_sb[:, p, :], h_old, ALU.mult).then_inc(rh_hi, 1)
                    nc.vector.tensor_tensor(rh[:, p, :], r_sb[:, p, :], h_old, ALU.mult).then_inc(rh_full, 1)
                    dve.wait_ge(rh_full, step + 1)
                    nc.vector.tensor_tensor(rh_p[:, p, 1, :], rh[:, p, :], rh_p[:, p, 0, :],
                                            ALU.subtract).then_inc(rh_lo, 1)
                    dve.wait_ge(z_made, step + 1)
                    nc.vector.tensor_tensor(zh_p[:, q, 0, :], z_sb[:, p, :], h_old, ALU.mult).then_inc(zh_hi, 1)
                    nc.vector.tensor_tensor(zh[:, q, :], z_sb[:, p, :], h_old, ALU.mult).then_inc(zh_full, 1)
                    if experts and t == at["choice"]:
                        dve.wait_ge(top_made, 2 * k)
                    nc.vector.tensor_scalar(keep[:, p, :], z_sb[:, p, :], -1.0, 1.0,
                                            ALU.mult, ALU.add).then_inc(keep_made, 1)
                    dve.wait_ge(zh_full, step + 1)
                    nc.vector.tensor_tensor(zh_p[:, q, 1, :], zh[:, q, :], zh_p[:, q, 0, :],
                                            ALU.subtract).then_inc(zh_lo, 1)
                    if experts and t == 1:
                        y_high(k - 1)
                    if experts and t == at["choice"]:
                        best_expert(k - 1)
                    if last and t == 9:
                        last_y_high(0)
                    if ffn and t == 5:
                        x1_high(k + 1)
                    dve.wait_ge(keep_made, step + 1)
                    dve.wait_ge(cand_made, step + 1)
                    nc.vector.tensor_tensor(m_p[:, q, 0, :], keep[:, p, :], cand[:, p, :], ALU.mult).then_inc(m_hi, 1)
                    nc.vector.tensor_tensor(m[:, q, :], keep[:, p, :], cand[:, p, :], ALU.mult).then_inc(m_full, 1)
                    dve.wait_ge(m_full, step + 1)
                    nc.vector.tensor_tensor(m_p[:, q, 1, :], m[:, q, :], m_p[:, q, 0, :],
                                            ALU.subtract).then_inc(m_lo, 1)
                    if experts and t == at["best"] and not last:
                        dve.wait_ge(logits_made, k)
                    nc.vector.tensor_tensor(h_new, zh[:, q, :], m[:, q, :], ALU.add).then_inc(h_made, 1)
                    if fin and t == 0:
                        finish(k - 2, par)
                    if experts and t == at["logits"]:
                        logits(k - 1)
                    if last and t == at["best"]:
                        dve.wait_ge(logits_made, k)
                    if ffn and t == 4:
                        x1_evacuate(k + 1)
                    if last and t == 12:
                        make_last_masks(0)
                    if experts:
                        if t == 1:
                            y_low(k - 1)
                        if t == at["best"]:
                            best_logit(k - 1)
                        if t == at["penalties"]:
                            penalties(k - 1)
                        if t == at["turn"]:
                            masks(k - 1)
                        if at["hidden"] <= t < at["hidden"] + NE:
                            expert_high(k - 1, t - at["hidden"])
                    if more_g and t == 9:
                        g_high(k + 2)
                    if first:
                        router_constants(t)
                    if fin and more_g and 10 <= t < 15:
                        bias1_parts(k - 2, t - 10)
                    if last and t == 9:
                        last_y_low(0)
                    if last and t == 10:
                        last_best_logit(0)
                    if last and t == 11:
                        last_best_expert(0)
                        last_penalties(0)
                    if last and 13 <= t < 15:
                        last_low(0, 2 * (t - 13))

            dve.wait_ge(router_in, 16)
            gru_chunk(0, 0, True, False, True, False, True)
            gru_chunk(1, 1, False, True, True, False, True)
            with dve.Fori(1, K // 2 - 1) as j:
                gru_chunk(2 * j, 0, False, True, True, True, True)
                gru_chunk(2 * j + 1, 1, False, True, True, True, True)
            gru_chunk(K - 2, 0, False, True, True, True, False)
            gru_chunk(K - 1, (K - 1) % 2, False, True, False, True, False, last=True)
            last_low(0, 4)
            last_y_high(1)
            last_y_low(1)
            last_low(0, 6)
            last_best_logit(1)
            last_best_expert(1)
            last_penalties(1)
            finish(K - 2, K % 2)
            make_last_masks(1)
            last_finish(0)
            for c in range(0, NE, 2):
                last_low(1, c)
            last_finish(1)

        @block.tensor
        def _(pe):
            mm = nc.tensor.matmul

            def three(out, w_hi, w_lo, a_hi, a_lo, stop, wait_lo=None, start=False):
                mm(out, w_lo, a_hi, start=start, stop=False)
                mm(out, w_hi, a_hi, start=False, stop=False)
                if wait_lo:
                    pe.wait_ge(*wait_lo)
                return mm(out, w_hi, a_lo, start=False, stop=stop)

            def ffn_hidden(n, j):
                if j >= 2:
                    pe.wait_ge(ffn_relu, n * NF + j - 1)
                w = wq16[:, 0, j * 128:(j + 1) * 128]
                mm(F_bank[j % 2][:, 0:N], w, g_hi[:, cols(n)], start=True, stop=False)
                mm(F_bank[j % 2][:, 0:N], w, g_lo[:, cols(n)], start=False, stop=True).then_inc(ffn_hid_mm, 1)

            def ffn_out(n, j):
                w = wq16[:, 1, j * 128:(j + 1) * 128]
                pe.wait_ge(ffn_hi, (n - 1) * NF + j + 1)
                mm(O_bank[:, 0:N], w, hid_hi[:, j, :], start=(j == 0), stop=False)
                pe.wait_ge(ffn_lo, (n - 1) * NF + j + 1)
                i = mm(O_bank[:, 0:N], w, hid_lo[:, j, :], start=False, stop=(j == NF - 1))
                if j == NF - 1:
                    i.then_inc(ffn_out_mm, 1)

            def projection(par, gate):
                return [R_bank[par][:, 0:N], ZH_bank[par][:, 0:N], ZH_bank[par][:, N:2 * N]][gate]

            def project_bias(par, gate):
                mm(projection(par, gate), gbias3[:, gate * C:(gate + 1) * C], ones3[:], start=(gate < 2), stop=False,
                   skip_group_check=True)

            def project_first(gate):
                mm(projection(0, gate), gru_sb[:, WXR + gate, :], x1[:, cols(0)], start=False, stop=False,
                   skip_group_check=True)

            def project_high(n, par, gate):
                if gate == 0:
                    pe.wait_ge(x1_hi_made, n)
                mm(projection(par, gate), gru_lo[:, WXR + gate, :], x1_hi[:], start=False, stop=False,
                   skip_group_check=True)
                mm(projection(par, gate), gru_hi[:, WXR + gate, :], x1_hi[:], start=False, stop=False,
                   skip_group_check=True)

            def project_low(n, par, gate):
                if gate == 0:
                    pe.wait_ge(x1_lo_made, n)
                mm(projection(par, gate), gru_hi[:, WXR + gate, :], x1_lo[:], start=False, stop=False,
                   skip_group_check=True)

            def whq(q, par, half):
                at = slice(half * (N // 2), (half + 1) * (N // 2))
                i = mm(L_bank[:, at], gru_sb[:, WHQ, :], hist[:, par, at], start=True, stop=True)
                if half == 1:
                    i.then_inc(whq_mm, 1)

            def router_logits(q):
                pe.wait_ge(y_lo_made, q + 1)
                for i in range(2):
                    out, tok = L_bank[:, N + i * E:N + (i + 1) * E], slice(i * 128, (i + 1) * 128)
                    mm(out, y_lo[:, tok], router_hi[:], start=True, stop=False)
                    mm(out, y_hi[:, tok], router_hi[:], start=False, stop=False)
                    ins = mm(out, y_hi[:, tok], router_lo[:], start=False, stop=True)
                ins.then_inc(logit_mm, 1)

            def turn_masks(q):
                pe.wait_ge(pen_made, 2 * q + 2)
                for i in range(2):
                    ins = nc.tensor.transpose(maskT_ps[0:96, i * 128:(i + 1) * 128], pen[:, i, :], ident[:])
                ins.then_inc(turn_mm, 1)

            def expert_hidden(q, c):
                if c >= 2:
                    pe.wait_ge(exp_relu, q * NE + c - 1)
                block_c = slice(c * 128, (c + 1) * 128)
                three(F_bank[c % 2][:, 0:N], w1_hi[:, block_c], w1_lo[:, block_c], y_hi[:], y_lo[:], False, start=True)
                if c == 0:
                    pe.wait_ge(masks_made, 2 * q + 1)
                mm(F_bank[c % 2][:, 0:N], expand_off[0:E, block_c], penT[:], start=False,
                   stop=True).then_inc(exp_hid_mm, 1)

            def expert_bias2(q):
                pe.wait_ge(masks_made, 2 * q + 2)
                mm(O_bank[:, 0:N], bias2_3[:], maskT[:], start=True, stop=False)

            def expert_out(q, c):
                pe.wait_ge(exp_hi, q * NE + c + 1)
                three(O_bank[:, 0:N], w2_hi[:, c, :], w2_lo[:, c, :], hid_hi[:, c % 4, :], hid_lo[:, c % 4, :],
                      c == NE - 1, (exp_lo, q * NE + c + 1)).then_inc(exp_out_mm, 1)

            def last_whq(h):
                mm(L_bank[:, 0:128], gru_sb[:, WHQ, :], hist[:, (K - 1) % 2, h * 128:(h + 1) * 128],
                   start=True, stop=True).then_inc(last_y_mm, 1)

            def last_router_logits(h):
                pe.wait_ge(last_y_lo, h + 1)
                out = L_bank[:, N:N + E]
                mm(out, y_last_lo[:, h, :], router_hi[:], start=True, stop=False)
                mm(out, y_last_hi[:, h, :], router_hi[:], start=False, stop=False)
                mm(out, y_last_hi[:, h, :], router_lo[:], start=False, stop=True).then_inc(last_logit_mm, 1)

            def last_turn_masks(h):
                pe.wait_ge(last_pen, h + 1)
                nc.tensor.transpose(maskT_ps[0:96, 0:128], pen_last[:, h, :], ident[:]).then_inc(last_turn_mm, 1)

            def last_hidden(h, c):
                if h == 1 and c % 2 == 0:
                    pe.wait_ge(last_lo, c // 2 + 1)
                out = last_hid_bank[c // 2][:, (c % 2) * 128:(c % 2 + 1) * 128]
                block_c = slice(c * 128, (c + 1) * 128)
                three(out, w1_hi[:, block_c], w1_lo[:, block_c], y_last_hi[:, h, :], y_last_lo[:, h, :],
                      False, start=True)
                if c == 0:
                    pe.wait_ge(last_masks, 2 * h + 2)
                mm(out, expand_off[:, block_c], penT_last[:, h, :], start=False, stop=True).then_inc(last_hid_mm, 1)

            def last_out(h, c):
                out = last_out_bank[h][:, 0:128]
                if c == 0:
                    mm(out, bias2_3[:], maskT_last[:, h, :], start=True, stop=False)
                if c % 2 == 0:
                    pe.wait_ge(last_lo, (h * NE + c) // 2 + 1)
                ins = three(out, w2_hi[:, c, :], w2_lo[:, c, :], hid_last_hi[:, h, c, :],
                            hid_last_lo[:, h, c, :], c == NE - 1)
                if c == NE - 1:
                    ins.then_inc(last_out_mm, 1)

            def product(out, gate, part, low=False):
                if not low:
                    mm(out, gru_lo[:, WHR + gate, :], part, start=False, stop=False, skip_group_check=True)
                return mm(out, gru_hi[:, WHR + gate, :], part, start=False, stop=low, skip_group_check=True)

            def low_rank(i):
                for b in range(4 * i, 4 * i + 4):
                    ins = mm(vv_bank[i][:, (b % 4) * C:(b % 4 + 1) * C], v_sb[:, b, :], v_sb[:, b, :],
                             start=True, stop=True)
                ins.then_inc(vv_mm, 1)

            def pre_product(i):
                seqs = PRE_GROUPS[i]
                pe.wait_ge(weff_made, seqs.start // 4 + 1)
                pe.wait_ge(x_in[seqs.start // 4], 16)
                for j, b in enumerate(seqs):
                    ins = mm(pre_bank[i][:, j * T:(j + 1) * T], weff[:, b, :], x_sb[:, b, :],
                             start=True, stop=True)
                ins.then_inc(pre_mm, 1)

            pe.wait_ge(v_first_in, 16)
            low_rank(0)
            pe.wait_ge(v_in, 16)
            for i in range(1, 4):
                low_rank(i)
            pe.wait_ge(asum_made, 1)
            pe.wait_ge(ones_set, 2)
            mm(F_bank[0][:, 0:2], ones[:], asum[:], start=True, stop=True).then_inc(gamma_mm, 1)
            for i in range(len(PRE_GROUPS)):
                pre_product(i)
            pe.wait_ge(below_made, 1)
            for _ in range(KEEP_WARM):
                mm(F_bank[1][:], below[:, 0, 0:128], below[:, 0, :], start=True, stop=True)
            pe.wait_ge(g_made, len(PRE_GROUPS))
            pe.wait_ge(wq_made, 1)

            def first_hidden(j):
                if j >= 2:
                    pe.wait_ge(ffn_relu, j - 1)
                mm(F_bank[j % 2][:, 0:N], wq[:, 0, j * 128:(j + 1) * 128], g[:, cols(0)],
                   start=True, stop=True).then_inc(ffn_hid_mm, 1)

            def first_out(j):
                pe.wait_ge(ffn_relu, j + 1)
                mm(O_bank[:, 0:N], wq[:, 1, j * 128:(j + 1) * 128], hid[:, j % 2, :],
                   start=(j == 0), stop=(j == NF - 1)).then_inc(ffn0_out, 1)

            first_hidden(0)
            first_hidden(1)
            pe.wait_ge(wq_made, 2)
            for j in range(NF):
                first_out(j)
                if j + 2 < NF:
                    first_hidden(j + 2)
            pe.wait_ge(gru_in, 16)
            pe.wait_ge(gb_step, 10)
            for gate in range(GATES):
                project_bias(0, gate)
            pe.wait_ge(x1_made, 1)
            project_first(0)
            pe.wait_ge(gru_lo_made, 1)
            pe.wait_ge(wq16_made, 1)

            def gru_chunk(k, par, first, experts, ffn, fin, last=False):
                when = LAST_STEPS if last else EXPERT_STEPS
                for t in range(STEPS):
                    q = t % 2
                    step = k * STEPS + t
                    at = slice(t * B, (t + 1) * B)
                    r_out, z_out = R_bank[par][:, at], ZH_bank[par][:, at]
                    if ffn and t == 0:
                        pe.wait_ge(g_lo_made, k + 1)
                    if not (first and t == 0):
                        pe.wait_ge(zh_lo, step)
                        product(r_out, 0, zh_p[:, q, 0, :])
                        product(r_out, 0, zh_p[:, q, 1, :], low=True)
                    pe.wait_ge(m_hi, step + 1)
                    product(r_out, 0, m_p[:, q, 0, :])
                    if not (first and t == 0):
                        product(z_out, 1, zh_p[:, q, 0, :])
                        product(z_out, 1, zh_p[:, q, 1, :], low=True)
                        product(z_out, 1, m_p[:, q, 0, :])
                    pe.wait_ge(m_lo, step + 1)
                    product(r_out, 0, m_p[:, q, 1, :], low=True).then_inc(r_mm, 1)
                    if first and t == 0:
                        project_first(1)
                        project_first(2)
                        product(z_out, 1, m_p[:, q, 0, :])
                    product(z_out, 1, m_p[:, q, 1, :], low=True).then_inc(z_mm, 1)
                    if ffn and t < NF:
                        ffn_hidden(k + 1, t)
                    if experts and t == 0:
                        whq(k - 1, 1 - par, 0)
                    if fin and t == 1:
                        pe.wait_ge(res_made, k - 1)
                    if ffn and t == 4:
                        for gate in range(GATES):
                            project_bias(1 - par, gate)
                    if ffn and t == 6:
                        project_high(k + 1, 1 - par, 0)
                    if experts and t == when["turn"]:
                        turn_masks(k - 1)
                    if experts and when["hidden"] <= t < when["hidden"] + NE:
                        expert_hidden(k - 1, t - when["hidden"])
                    if ffn and t == 15:
                        project_high(k + 1, 1 - par, 2)
                        project_low(k + 1, 1 - par, 2)
                    if last and t == 10:
                        last_router_logits(0)
                    if last and 13 <= t:
                        last_hidden(0, 2 * (t - 13))
                        last_hidden(0, 2 * (t - 13) + 1)
                    pe.wait_ge(z_made, step + 1)
                    pe.wait_ge(rh_hi, step + 1)
                    c_out = ZH_bank[par][:, N + t * B:N + (t + 1) * B]
                    product(c_out, 2, rh_p[:, q, 0, :])
                    pe.wait_ge(rh_lo, step + 1)
                    product(c_out, 2, rh_p[:, q, 1, :], low=True).then_inc(cand_mm, 1)
                    if experts and t == 0:
                        whq(k - 1, 1 - par, 1)
                    if experts and t == when["logits"]:
                        router_logits(k - 1)
                    if ffn and 1 <= t < 1 + NF:
                        ffn_out(k + 1, t - 1)
                    if ffn and t == 6:
                        project_low(k + 1, 1 - par, 0)
                        project_high(k + 1, 1 - par, 1)
                    if ffn and t == 7:
                        project_low(k + 1, 1 - par, 1)
                    if experts and t == when["hidden"]:
                        expert_bias2(k - 1)
                    if last and t == 12:
                        last_turn_masks(0)
                    out_block = t - when["hidden"] - (2 if last and t > 8 else 1)
                    if experts and 0 <= out_block < NE and not (last and t == 8):
                        expert_out(k - 1, out_block)
                    if last and t == 15:
                        last_hidden(0, 6)
                        last_hidden(0, 7)
                    if last and t == 8:
                        last_whq(0)

            gru_chunk(0, 0, True, False, True, False)
            for s, n in ((ident_made, 1), (expand_made, 2), (w_lo_made, 3), (b2_step, 8)):
                pe.wait_ge(s, n)
            gru_chunk(1, 1, False, True, True, False)
            with pe.Fori(1, K // 2 - 1) as j:
                gru_chunk(2 * j, 0, False, True, True, True)
                gru_chunk(2 * j + 1, 1, False, True, True, True)
            gru_chunk(K - 2, 0, False, True, True, True)
            pe.wait_ge(b1_rows, 48)
            pe.wait_ge(b1_ones, 1)
            gru_chunk(K - 1, (K - 1) % 2, False, True, False, True, last=True)
            pe.wait_ge(h_made, K * STEPS + 1)
            last_whq(1)
            for c in range(4):
                last_out(0, c)
            last_router_logits(1)
            for c in range(4, NE):
                last_out(0, c)
            last_turn_masks(1)
            for c in range(6):
                last_hidden(1, c)
            last_hidden(1, 6)
            last_hidden(1, 7)
            for c in range(NE):
                last_out(1, c)


def kernel(x, fside_Bx1x1024x16_0, cond_1024, L0_cond_W, L0_cond_fc_bias, L0_ffn_W1, L0_ffn_b1,
           L0_ffn_W2, L0_ffn_b2, L1_cond_Wxz, L1_cond_bxz, L1_cond_Whz, L1_cond_bhz, L1_cond_Wxr,
           L1_cond_bxr, L1_cond_Whr, L1_cond_bhr, L1_cond_Wxh, L1_cond_bxh, L1_cond_Whh, L1_cond_bhh,
           L1_cond_Whq, L1_cond_bhq, L1_ffn_router_w, L1_ffn_router_b, L1_ffn_weights1,
           L1_ffn_bias1, L1_ffn_weights2, L1_ffn_bias2):
    import concourse.bacc as bacc
    from concourse.bass_utils import run_bass_kernel_spmd

    a = np.asarray
    f32 = np.float32
    rows = [a(L0_cond_fc_bias)[None], a(cond_1024), a(L0_ffn_b1).reshape(NF, 128), a(L0_ffn_b2)[None],
            a(L1_cond_bhq)[None], a(L1_ffn_bias1).reshape(NE, 128)]
    arrays = {
        "xT": a(x).transpose(2, 0, 1),
        "vT": a(fside_Bx1x1024x16_0)[:, 0].transpose(2, 0, 1),
        "early": a(L0_cond_W).T,
        "vectors": np.concatenate(rows, 0).T,
        "ffn": np.stack([a(L0_ffn_W1).T, a(L0_ffn_W2).T.reshape(NF, 128, C).transpose(1, 0, 2).reshape(128, FF)], 1),
        "gru": np.stack([a(w).T for w in (L1_cond_Wxr, L1_cond_Wxz, L1_cond_Wxh, L1_cond_Whr,
                                          L1_cond_Whz, L1_cond_Whh, L1_cond_Whq)], 1),
        "gate_bias": np.stack([np.stack([np.stack([a(L1_cond_bxr), a(L1_cond_bxz), a(L1_cond_bxh)]),
                                         np.stack([a(L1_cond_bhr), a(L1_cond_bhz), a(L1_cond_bhh)])])] * 3),
        "consts": np.concatenate([np.eye(128, dtype=f32), np.tile(np.arange(E, dtype=f32), (128, 3)),
                                  np.eye(128, 3, dtype=f32)], 1),
        "expand": np.repeat(np.eye(E, dtype=f32), HE, axis=1),
        "router": np.stack([a(L1_ffn_router_w).T, np.stack([a(L1_ffn_router_b)] * 128)], 1),
        "w1": a(L1_ffn_weights1).transpose(1, 0, 2).reshape(C, E * HE),
        "w2": a(L1_ffn_weights2).reshape(NE, 128, C).transpose(1, 0, 2),
        "bias1": a(L1_ffn_bias1).reshape(1, E * HE),
        "bias2": np.concatenate([a(L1_ffn_bias2)] * 3, 0),
    }
    arrays = {n: np.ascontiguousarray(v) for n, v in arrays.items()}

    nc = bacc.Bacc("TRN2", target_bir_lowering=False, num_devices=1)
    args = [nc.dram_tensor(n, v.shape, mybir.dt.from_np(v.dtype), kind="ExternalInput").ap()
            for n, v in arrays.items()]
    out = nc.dram_tensor("outT", (C, T * B), F32, kind="ExternalOutput").ap()
    build(nc, *args, out)
    r = run_bass_kernel_spmd(nc, [arrays], core_ids=[0])
    return np.ascontiguousarray(a(r.results[0]["outT"]).reshape(C, T, B).transpose(2, 1, 0))
```
